# Optimizing a Trainium2 kernel written in Bass

```python
import numpy as np
import jax
import jax.numpy as jnp

def _softmax(x, axis=-1):
    return jax.nn.softmax(x, axis=axis)

def _gelu(x):
    return jax.nn.gelu(x, approximate=True)

def _silu(x):
    return jax.nn.silu(x)

def _sigmoid(x):
    return jax.nn.sigmoid(x)

def _layernorm(x, axis=-1, eps=1e-05):
    m = jnp.mean(x, axis=axis, keepdims=True)
    v = jnp.var(x, axis=axis, keepdims=True)
    return (x - m) / jnp.sqrt(v + eps)

def _scatter_add(tgt, idx, src, axis=0):
    return tgt.at[idx].add(src)

def _segment_sum(src, seg, n):
    return jax.ops.segment_sum(src, seg, n)
kernel_name = 'mk_sandwich_d2_jaxref_r8_4416d3'

def setup_inputs(seed: int=0):
    np.random.seed(seed)
    _w = jnp.asarray

    def _L0_attn_setup():
        import jax, jax.numpy as jnp
        import numpy as np
        from jax import lax
        H_SIZE = 256
        NUM_K = 16
        NUM_V = 32
        DK = 128
        DV = 128
        KDIM = NUM_K * DK
        VDIM = NUM_V * DV
        KCONV = 4
        RMS_EPS = 1e-06
        L2_EPS = 1e-06

        def l2norm(x, eps=L2_EPS):
            return x * lax.rsqrt(jnp.sum(x * x, axis=-1, keepdims=True) + eps)

        def _forward(hidden_states, w_qkvz, w_ba, conv_w, dt_bias, A_log, norm_w, w_out):
            B, S, _ = hidden_states.shape
            rf = NUM_V // NUM_K
            qkvz = hidden_states @ w_qkvz
            ba = hidden_states @ w_ba
            qkvz = qkvz.reshape(B, S, NUM_K, 2 * DK + 2 * rf * DV)
            q, k, v, z = jnp.split(qkvz, [DK, 2 * DK, 2 * DK + rf * DV], axis=3)
            ba = ba.reshape(B, S, NUM_K, 2 * rf)
            b, a = jnp.split(ba, [rf], axis=3)
            v = v.reshape(B, S, NUM_V, DV)
            z = z.reshape(B, S, NUM_V, DV)
            b = b.reshape(B, S, NUM_V)
            a = a.reshape(B, S, NUM_V)
            mixed = jnp.concatenate([q.reshape(B, S, KDIM), k.reshape(B, S, KDIM), v.reshape(B, S, VDIM)], axis=-1)
            x = mixed.transpose(0, 2, 1)
            x = jnp.pad(x, ((0, 0), (0, 0), (KCONV - 1, 0)))
            x = lax.conv_general_dilated(x, conv_w, window_strides=(1,), padding='VALID', feature_group_count=x.shape[1])
            x = jax.nn.silu(x).transpose(0, 2, 1)
            q, k, v = jnp.split(x, [KDIM, 2 * KDIM], axis=-1)
            q = q.reshape(B, S, NUM_K, DK)
            k = k.reshape(B, S, NUM_K, DK)
            v = v.reshape(B, S, NUM_V, DV)
            beta = jax.nn.sigmoid(b)
            g = -jnp.exp(A_log) * jax.nn.softplus(a + dt_bias)
            if rf > 1:
                q = jnp.repeat(q, rf, axis=2)
                k = jnp.repeat(k, rf, axis=2)
            q = l2norm(q) * DK ** (-0.5)
            k = l2norm(k)
            S0 = jnp.zeros((B, NUM_V, DK, DV), q.dtype)

            def step(state, inp):
                q_t, k_t, v_t, g_t, b_t = inp
                state = state * jnp.exp(g_t)[..., None, None]
                kv_mem = jnp.einsum('bhkv,bhk->bhv', state, k_t)
                delta = (v_t - kv_mem) * b_t[..., None]
                state = state + jnp.einsum('bhk,bhv->bhkv', k_t, delta)
                o = jnp.einsum('bhkv,bhk->bhv', state, q_t)
                return (state, o)
            xs = (jnp.moveaxis(q, 1, 0), jnp.moveaxis(k, 1, 0), jnp.moveaxis(v, 1, 0), jnp.moveaxis(g, 1, 0), jnp.moveaxis(beta, 1, 0))
            _, out = lax.scan(step, S0, xs)
            out = jnp.moveaxis(out, 0, 1)
            xg = out * jax.nn.silu(z)
            y = xg * lax.rsqrt(jnp.mean(xg * xg, axis=-1, keepdims=True) + RMS_EPS) * norm_w
            y = y.reshape(B, S, VDIM)
            return y @ w_out
        key = jax.random.key(seed)
        ks = jax.random.split(key, 7)
        B, S = (2, 128)
        conv_dim = 2 * KDIM + VDIM
        return {'hidden_states': jax.random.normal(ks[0], (B, S, H_SIZE), jnp.float32), 'w_qkvz': jax.random.normal(ks[1], (H_SIZE, 2 * KDIM + 2 * VDIM), jnp.float32) * 0.02, 'w_ba': jax.random.normal(ks[2], (H_SIZE, 2 * NUM_V), jnp.float32) * 0.02, 'conv_w': jax.random.normal(ks[3], (conv_dim, 1, KCONV), jnp.float32) * 0.2, 'dt_bias': jnp.ones((NUM_V,), jnp.float32), 'A_log': jnp.log(jax.random.uniform(ks[4], (NUM_V,), jnp.float32, 0.5, 8.0)), 'norm_w': jnp.ones((DV,), jnp.float32), 'w_out': jax.random.normal(ks[5], (VDIM, H_SIZE), jnp.float32) * 0.02}
    _L0_attn_in = _L0_attn_setup()

    def _L0_ffn_setup():
        import jax, jax.numpy as jnp
        import numpy as np
        CAPACITY = 0.125
        HEAD_DIM = 128
        N_HEADS = 16
        N_KV_HEADS = 8
        ROPE_THETA = 10000.0
        EPS = 1e-06

        def _rms_norm(x, w):
            return x * jax.lax.rsqrt(jnp.mean(x * x, axis=-1, keepdims=True) + EPS) * w

        def _rotate_half(t):
            h = t.shape[-1] // 2
            return jnp.concatenate([-t[..., h:], t[..., :h]], axis=-1)
        key = jax.random.key(seed)
        ks = jax.random.split(key, 12)
        B, T, D = (4, 512, 256)
        I = 1024
        s = 0.02
        return {'hidden_states': jax.random.normal(ks[0], (B, T, D), jnp.float32), 'w_router': jax.random.normal(ks[1], (D,), jnp.float32) * s, 'wq': jax.random.normal(ks[2], (D, N_HEADS * HEAD_DIM), jnp.float32) * s, 'bq': jnp.zeros((N_HEADS * HEAD_DIM,), jnp.float32), 'wk': jax.random.normal(ks[3], (D, N_KV_HEADS * HEAD_DIM), jnp.float32) * s, 'bk': jnp.zeros((N_KV_HEADS * HEAD_DIM,), jnp.float32), 'wv': jax.random.normal(ks[4], (D, N_KV_HEADS * HEAD_DIM), jnp.float32) * s, 'bv': jnp.zeros((N_KV_HEADS * HEAD_DIM,), jnp.float32), 'wo': jax.random.normal(ks[5], (N_HEADS * HEAD_DIM, D), jnp.float32) * s, 'w_gate': jax.random.normal(ks[6], (D, I), jnp.float32) * s, 'w_up': jax.random.normal(ks[7], (D, I), jnp.float32) * s, 'w_down': jax.random.normal(ks[8], (I, D), jnp.float32) * s, 'ln1_w': jnp.ones((D,), jnp.float32), 'ln2_w': jnp.ones((D,), jnp.float32)}
    _L0_ffn_in = _L0_ffn_setup()

    def _L1_attn_setup():
        import jax, jax.numpy as jnp
        import numpy as np
        B, N, D, BS = (2, 512, 256, 32)

        def rms_norm(x):
            eps = jnp.asarray(jnp.finfo(x.dtype).eps, x.dtype)
            return x * jax.lax.rsqrt(jnp.mean(x * x, axis=-1, keepdims=True) + eps)

        def la_kernel(q, k, v, bs):
            b, n, d = q.shape
            T = n // bs
            qc = q.reshape(b, T, bs, d).transpose(1, 0, 2, 3)
            kc = k.reshape(b, T, bs, d).transpose(1, 0, 2, 3)
            vc = v.reshape(b, T, bs, d).transpose(1, 0, 2, 3)
            mask = jnp.tril(jnp.ones((bs, bs), q.dtype))

            def step(kv, qkv):
                qt, kt, vt = qkv
                s = jnp.einsum('bid,bjd->bij', qt, kt) * mask
                ot = jnp.einsum('bij,bjd->bid', s, vt) + jnp.einsum('bid,bde->bie', qt, kv)
                kv = kv + jnp.einsum('bjd,bje->bde', kt, vt)
                return (kv, ot)
            kv0 = jnp.zeros((b, d, d), q.dtype)
            _, o = jax.lax.scan(step, kv0, (qc, kc, vc))
            return o.transpose(1, 0, 2, 3).reshape(b, n, d)
        key = jax.random.key(seed)
        ks = jax.random.split(key, 6)
        scale = 0.02
        x = jax.random.normal(ks[0], (B, N, D), jnp.float32)
        Wq = jax.random.normal(ks[1], (D, D), jnp.float32) * scale
        Wk = jax.random.normal(ks[2], (D, D), jnp.float32) * scale
        Wv = jax.random.normal(ks[3], (D, D), jnp.float32) * scale
        Wg = jax.random.normal(ks[4], (D, D), jnp.float32) * scale
        Wp = jax.random.normal(ks[5], (D, D), jnp.float32) * scale
        return {'x': x, 'Wq': Wq, 'Wk': Wk, 'Wv': Wv, 'Wg': Wg, 'Wp': Wp}
    _L1_attn_in = _L1_attn_setup()

    def _L1_ffn_setup():
        import jax, jax.numpy as jnp
        import numpy as np
        K_TOP = 2
        key = jax.random.key(seed)
        ks = jax.random.split(key, 6)
        s = 0.02
        B, S, H, D = (4, 128, 256, 128)
        E_SH, E_RT = (2, 16)
        return {'x': jax.random.normal(ks[0], (B, S, H), dtype=jnp.float32), 'Wsh_up': jax.random.normal(ks[1], (E_SH, H, D), dtype=jnp.float32) * s, 'Wsh_down': jax.random.normal(ks[2], (E_SH, D, H), dtype=jnp.float32) * s, 'Wrt_up': jax.random.normal(ks[3], (E_RT, H, D), dtype=jnp.float32) * s, 'Wrt_down': jax.random.normal(ks[4], (E_RT, D, H), dtype=jnp.float32) * s, 'W_router': jax.random.normal(ks[5], (H, E_RT), dtype=jnp.float32) * s}
    _L1_ffn_in = _L1_ffn_setup()
    _d = {'L0_attn_hidden_states': _L0_attn_in['hidden_states'], 'L0_attn_w_qkvz': _L0_attn_in['w_qkvz'], 'L0_attn_w_ba': _L0_attn_in['w_ba'], 'L0_attn_conv_w': _L0_attn_in['conv_w'], 'L0_attn_dt_bias': _L0_attn_in['dt_bias'], 'L0_attn_A_log': _L0_attn_in['A_log'], 'L0_attn_norm_w': _L0_attn_in['norm_w'], 'L0_attn_w_out': _L0_attn_in['w_out'], 'L0_ffn_w_router': _L0_ffn_in['w_router'], 'L0_ffn_wq': _L0_ffn_in['wq'], 'L0_ffn_bq': _L0_ffn_in['bq'], 'L0_ffn_wk': _L0_ffn_in['wk'], 'L0_ffn_bk': _L0_ffn_in['bk'], 'L0_ffn_wv': _L0_ffn_in['wv'], 'L0_ffn_bv': _L0_ffn_in['bv'], 'L0_ffn_wo': _L0_ffn_in['wo'], 'L0_ffn_w_gate': _L0_ffn_in['w_gate'], 'L0_ffn_w_up': _L0_ffn_in['w_up'], 'L0_ffn_w_down': _L0_ffn_in['w_down'], 'L0_ffn_ln1_w': _L0_ffn_in['ln1_w'], 'L0_ffn_ln2_w': _L0_ffn_in['ln2_w'], 'L1_attn_Wq': _L1_attn_in['Wq'], 'L1_attn_Wk': _L1_attn_in['Wk'], 'L1_attn_Wv': _L1_attn_in['Wv'], 'L1_attn_Wg': _L1_attn_in['Wg'], 'L1_attn_Wp': _L1_attn_in['Wp'], 'L1_ffn_Wsh_up': _L1_ffn_in['Wsh_up'], 'L1_ffn_Wsh_down': _L1_ffn_in['Wsh_down'], 'L1_ffn_Wrt_up': _L1_ffn_in['Wrt_up'], 'L1_ffn_Wrt_down': _L1_ffn_in['Wrt_down'], 'L1_ffn_W_router': _L1_ffn_in['W_router']}
    _x0 = _d['L0_attn_hidden_states']
    _d['L0_attn_hidden_states'] = jax.random.normal(jax.random.fold_in(jax.random.key(seed), 1), (4, 256, 256), dtype=_x0.dtype)
    del _x0
    return _d

def reference(L0_attn_hidden_states, L0_attn_w_qkvz, L0_attn_w_ba, L0_attn_conv_w, L0_attn_dt_bias, L0_attn_A_log, L0_attn_norm_w, L0_attn_w_out, L0_ffn_w_router, L0_ffn_wq, L0_ffn_bq, L0_ffn_wk, L0_ffn_bk, L0_ffn_wv, L0_ffn_bv, L0_ffn_wo, L0_ffn_w_gate, L0_ffn_w_up, L0_ffn_w_down, L0_ffn_ln1_w, L0_ffn_ln2_w, L1_attn_Wq, L1_attn_Wk, L1_attn_Wv, L1_attn_Wg, L1_attn_Wp, L1_ffn_Wsh_up, L1_ffn_Wsh_down, L1_ffn_Wrt_up, L1_ffn_Wrt_down, L1_ffn_W_router):

    def _L0_attn_ref(hidden_states, w_qkvz, w_ba, conv_w, dt_bias, A_log, norm_w, w_out):
        import jax, jax.numpy as jnp
        import numpy as np
        from jax import lax
        H_SIZE = 256
        NUM_K = 16
        NUM_V = 32
        DK = 128
        DV = 128
        KDIM = NUM_K * DK
        VDIM = NUM_V * DV
        KCONV = 4
        RMS_EPS = 1e-06
        L2_EPS = 1e-06

        def l2norm(x, eps=L2_EPS):
            return x * lax.rsqrt(jnp.sum(x * x, axis=-1, keepdims=True) + eps)

        def _forward(hidden_states, w_qkvz, w_ba, conv_w, dt_bias, A_log, norm_w, w_out):
            B, S, _ = hidden_states.shape
            rf = NUM_V // NUM_K
            qkvz = hidden_states @ w_qkvz
            ba = hidden_states @ w_ba
            qkvz = qkvz.reshape(B, S, NUM_K, 2 * DK + 2 * rf * DV)
            q, k, v, z = jnp.split(qkvz, [DK, 2 * DK, 2 * DK + rf * DV], axis=3)
            ba = ba.reshape(B, S, NUM_K, 2 * rf)
            b, a = jnp.split(ba, [rf], axis=3)
            v = v.reshape(B, S, NUM_V, DV)
            z = z.reshape(B, S, NUM_V, DV)
            b = b.reshape(B, S, NUM_V)
            a = a.reshape(B, S, NUM_V)
            mixed = jnp.concatenate([q.reshape(B, S, KDIM), k.reshape(B, S, KDIM), v.reshape(B, S, VDIM)], axis=-1)
            x = mixed.transpose(0, 2, 1)
            x = jnp.pad(x, ((0, 0), (0, 0), (KCONV - 1, 0)))
            x = lax.conv_general_dilated(x, conv_w, window_strides=(1,), padding='VALID', feature_group_count=x.shape[1])
            x = jax.nn.silu(x).transpose(0, 2, 1)
            q, k, v = jnp.split(x, [KDIM, 2 * KDIM], axis=-1)
            q = q.reshape(B, S, NUM_K, DK)
            k = k.reshape(B, S, NUM_K, DK)
            v = v.reshape(B, S, NUM_V, DV)
            beta = jax.nn.sigmoid(b)
            g = -jnp.exp(A_log) * jax.nn.softplus(a + dt_bias)
            if rf > 1:
                q = jnp.repeat(q, rf, axis=2)
                k = jnp.repeat(k, rf, axis=2)
            q = l2norm(q) * DK ** (-0.5)
            k = l2norm(k)
            S0 = jnp.zeros((B, NUM_V, DK, DV), q.dtype)

            def step(state, inp):
                q_t, k_t, v_t, g_t, b_t = inp
                state = state * jnp.exp(g_t)[..., None, None]
                kv_mem = jnp.einsum('bhkv,bhk->bhv', state, k_t)
                delta = (v_t - kv_mem) * b_t[..., None]
                state = state + jnp.einsum('bhk,bhv->bhkv', k_t, delta)
                o = jnp.einsum('bhkv,bhk->bhv', state, q_t)
                return (state, o)
            xs = (jnp.moveaxis(q, 1, 0), jnp.moveaxis(k, 1, 0), jnp.moveaxis(v, 1, 0), jnp.moveaxis(g, 1, 0), jnp.moveaxis(beta, 1, 0))
            _, out = lax.scan(step, S0, xs)
            out = jnp.moveaxis(out, 0, 1)
            xg = out * jax.nn.silu(z)
            y = xg * lax.rsqrt(jnp.mean(xg * xg, axis=-1, keepdims=True) + RMS_EPS) * norm_w
            y = y.reshape(B, S, VDIM)
            return y @ w_out
        return _forward(hidden_states, w_qkvz, w_ba, conv_w, dt_bias, A_log, norm_w, w_out)

    def _L0_ffn_ref(hidden_states, w_router, wq, bq, wk, bk, wv, bv, wo, w_gate, w_up, w_down, ln1_w, ln2_w):
        import jax, jax.numpy as jnp
        import numpy as np
        CAPACITY = 0.125
        HEAD_DIM = 128
        N_HEADS = 16
        N_KV_HEADS = 8
        ROPE_THETA = 10000.0
        EPS = 1e-06

        def _rms_norm(x, w):
            return x * jax.lax.rsqrt(jnp.mean(x * x, axis=-1, keepdims=True) + EPS) * w

        def _rotate_half(t):
            h = t.shape[-1] // 2
            return jnp.concatenate([-t[..., h:], t[..., :h]], axis=-1)
        B, T, D = hidden_states.shape
        k = max(1, int(T * CAPACITY))
        scores = jnp.einsum('btd,d->bt', hidden_states, w_router)
        _, idx = jax.lax.top_k(scores, k)
        idx = jnp.sort(idx, axis=-1)
        b = jnp.arange(B)[:, None]
        sel = hidden_states[b, idx]
        sel_scores = scores[b, idx]
        S = B * k
        x = sel.reshape(S, D)
        pos = idx.reshape(S)
        inv_freq = 1.0 / ROPE_THETA ** (jnp.arange(0, HEAD_DIM, 2, dtype=jnp.float32) / HEAD_DIM)
        ang = pos.astype(jnp.float32)[:, None] * inv_freq
        cos = jnp.concatenate([jnp.cos(ang), jnp.cos(ang)], axis=-1)[:, None, :]
        sin = jnp.concatenate([jnp.sin(ang), jnp.sin(ang)], axis=-1)[:, None, :]
        h = _rms_norm(x, ln1_w)
        q = (h @ wq + bq).reshape(S, N_HEADS, HEAD_DIM)
        kk = (h @ wk + bk).reshape(S, N_KV_HEADS, HEAD_DIM)
        v = (h @ wv + bv).reshape(S, N_KV_HEADS, HEAD_DIM)
        q = q * cos + _rotate_half(q) * sin
        kk = kk * cos + _rotate_half(kk) * sin
        rep = N_HEADS // N_KV_HEADS
        kk = jnp.repeat(kk, rep, axis=1)
        v = jnp.repeat(v, rep, axis=1)
        att = jnp.einsum('shd,thd->hst', q, kk) / np.sqrt(HEAD_DIM)
        causal = jnp.tril(jnp.ones((S, S), bool))
        att = jnp.where(causal[None], att, jnp.finfo(att.dtype).min)
        att = jax.nn.softmax(att, axis=-1)
        attn_out = jnp.einsum('hst,thd->shd', att, v).reshape(S, N_HEADS * HEAD_DIM) @ wo
        x1 = x + attn_out
        h2 = _rms_norm(x1, ln2_w)
        mlp = jax.nn.silu(h2 @ w_gate) * (h2 @ w_up) @ w_down
        processed = x1 + mlp
        gate = jax.nn.sigmoid(sel_scores).reshape(S, 1)
        gated = gate * processed + (1.0 - gate) * x
        output = hidden_states.at[b, idx].set(gated.reshape(B, k, D))
        return output

    def _L1_attn_ref(x, Wq, Wk, Wv, Wg, Wp):
        import jax, jax.numpy as jnp
        import numpy as np
        B, N, D, BS = (2, 512, 256, 32)

        def rms_norm(x):
            eps = jnp.asarray(jnp.finfo(x.dtype).eps, x.dtype)
            return x * jax.lax.rsqrt(jnp.mean(x * x, axis=-1, keepdims=True) + eps)

        def la_kernel(q, k, v, bs):
            b, n, d = q.shape
            T = n // bs
            qc = q.reshape(b, T, bs, d).transpose(1, 0, 2, 3)
            kc = k.reshape(b, T, bs, d).transpose(1, 0, 2, 3)
            vc = v.reshape(b, T, bs, d).transpose(1, 0, 2, 3)
            mask = jnp.tril(jnp.ones((bs, bs), q.dtype))

            def step(kv, qkv):
                qt, kt, vt = qkv
                s = jnp.einsum('bid,bjd->bij', qt, kt) * mask
                ot = jnp.einsum('bij,bjd->bid', s, vt) + jnp.einsum('bid,bde->bie', qt, kv)
                kv = kv + jnp.einsum('bjd,bje->bde', kt, vt)
                return (kv, ot)
            kv0 = jnp.zeros((b, d, d), q.dtype)
            _, o = jax.lax.scan(step, kv0, (qc, kc, vc))
            return o.transpose(1, 0, 2, 3).reshape(b, n, d)
        xn = rms_norm(x)
        q = jax.nn.silu(jnp.einsum('bnd,od->bno', xn, Wq))
        k = jax.nn.silu(jnp.einsum('bnd,od->bno', xn, Wk))
        v = jax.nn.silu(jnp.einsum('bnd,od->bno', xn, Wv))
        g = jax.nn.sigmoid(jnp.einsum('bnd,od->bno', xn, Wg))
        o = la_kernel(q, k, v, BS) * g
        return jnp.einsum('bnd,od->bno', o, Wp)

    def _L1_ffn_ref(x, Wsh_up, Wsh_down, Wrt_up, Wrt_down, W_router):
        import jax, jax.numpy as jnp
        import numpy as np
        K_TOP = 2
        B, S, H = x.shape
        E_rt = Wrt_up.shape[0]
        xt = x.reshape(B * S, H)
        sh_mid = jax.nn.gelu(jnp.einsum('th,ehd->ted', xt, Wsh_up), approximate=False)
        shared_out = jnp.einsum('ted,edh->th', sh_mid, Wsh_down)
        probs = jax.nn.softmax(xt @ W_router, axis=-1)
        top_v, top_i = jax.lax.top_k(probs, K_TOP)
        gate = jnp.sum(jax.nn.one_hot(top_i, E_rt, dtype=xt.dtype) * top_v[..., None], axis=1)
        rt_mid = jax.nn.gelu(jnp.einsum('th,ehd->ted', xt, Wrt_up), approximate=False)
        routed_out = jnp.einsum('ted,edh->th', rt_mid * gate[:, :, None], Wrt_down)
        return (shared_out + routed_out).reshape(B, S, H)
    x = L0_attn_hidden_states
    x = x + _layernorm(_L0_attn_ref(_layernorm(x, axis=-1), L0_attn_w_qkvz, L0_attn_w_ba, L0_attn_conv_w, L0_attn_dt_bias, L0_attn_A_log, L0_attn_norm_w, L0_attn_w_out), axis=-1)
    x = x + _layernorm(_L0_ffn_ref(_layernorm(x, axis=-1), L0_ffn_w_router, L0_ffn_wq, L0_ffn_bq, L0_ffn_wk, L0_ffn_bk, L0_ffn_wv, L0_ffn_bv, L0_ffn_wo, L0_ffn_w_gate, L0_ffn_w_up, L0_ffn_w_down, L0_ffn_ln1_w, L0_ffn_ln2_w), axis=-1)
    x = x + _layernorm(_L1_attn_ref(_layernorm(x, axis=-1), L1_attn_Wq, L1_attn_Wk, L1_attn_Wv, L1_attn_Wg, L1_attn_Wp), axis=-1)
    x = x + _layernorm(_L1_ffn_ref(_layernorm(x, axis=-1), L1_ffn_Wsh_up, L1_ffn_Wsh_down, L1_ffn_Wrt_up, L1_ffn_Wrt_down, L1_ffn_W_router), axis=-1)
    return x

_drawn_inputs = setup_inputs


def setup_inputs(seed=0):
    import zlib

    import numpy as np

    out = dict(_drawn_inputs(seed))
    spreads = {'L0_attn_dt_bias': (1.0, 0.6),
     'L0_attn_norm_w': (1.0, 0.2),
     'L0_ffn_bq': (0.0, 0.8),
     'L0_ffn_bk': (0.0, 0.8),
     'L0_ffn_bv': (0.0, 0.76),
     'L0_ffn_ln1_w': (1.0, 0.6),
     'L0_ffn_ln2_w': (1.0, 0.6)}
    factors = {'L0_ffn_w_router': 4.376,
     'L0_ffn_wq': 8.0,
     'L0_ffn_wk': 8.0,
     'L0_ffn_wv': 5.889,
     'L0_ffn_wo': 4.182,
     'L0_ffn_w_gate': 8.0,
     'L0_ffn_w_up': 8.0,
     'L0_ffn_w_down': 8.0}
    for name, (base, spread) in spreads.items():
        noise = np.random.default_rng([zlib.crc32(name.encode()), seed]).standard_normal(out[name].shape)
        drawn = base * np.exp(spread * noise) if base else spread * noise
        out[name] = jnp.asarray(drawn.astype(out[name].dtype))
    for name, factor in factors.items():
        out[name] = (out[name] * factor).astype(out[name].dtype)
    return out
```

```python
from contextlib import ExitStack

import concourse.bass as bass
import numpy as np
from concourse import mybir

ACT = mybir.ActivationFunctionType
ALU = mybir.AluOpType
AX = mybir.AxisListType
F32 = mybir.dt.float32
F32R = mybir.dt.float32r
BF16 = mybir.dt.bfloat16
U32 = mybir.dt.uint32

P = 128
B, T, D = 4, 256, 256
NT = B * T // P
KD = D // P
LN_EPS = 1e-5

NK, RF, DK = 16, 2, 128
NV = NK * RF
HW = 2 * DK + 2 * RF * DK
NP = NT * RF
TAPS = 4
TOP = T // 8
BLK = 32
NSC = 5 * NP
BETA, LOGDECAY, NEGGAM, TAIL, GAM = (k * NP for k in range(5))


def tile_of(c, b):
    return 2 * b + c


def constant_parts():
    i = np.arange(P)
    eye = np.eye(P)
    upto = (i[:, None] <= i[None, :]) * 1.0
    after = (i[:, None] > i[None, :]) * 1.0
    below = np.where(i[None, :] < i[:, None], -30000.0, 0.0)
    j = np.arange(BLK)
    row = i % BLK
    strict = (row[:, None] < j[None, :]) * 1.0
    levels = []
    for b in (1, 2, 4, 8, 16):
        same = (row[:, None] // (2 * b)) == (j[None, :] // (2 * b))
        levels.append((same & ((row[:, None] // b) % 2 == 1) & ((j[None, :] // b) % 2 == 0)) * 1.0)
    eyec = np.tile((row[:, None] == j[None, :]) * 1.0, (1, 2))
    even = (((i // BLK) % 2) == 0)[:, None] * 1.0
    pows = np.concatenate([np.full((P, NT), 0.5), np.full((P, NT), -0.5)], 1)
    return {"eye": eye, "upto": upto, "after": after, "below": below, "strict": strict,
            "levels": np.concatenate(levels, 1), "eyec": eyec, "even": even, "odd": 1 - even,
            "pows": pows, "mhalf": np.full((P, NP), -0.5), "ones": np.ones((P, P)), "count": np.tile(np.arange(P), (P, 1)), "slot0": TOP * i[:, None],
            "causal": np.where(i[None, :] > i[:, None], -1e30, 0.0), "lmask": np.concatenate([upto, np.ones((P, P)), upto], 1)}


def packed_constants():
    parts = constant_parts()
    at, n = {}, 0
    for k, v in parts.items():
        at[k] = (n, n + v.shape[1])
        n += v.shape[1]
    return np.concatenate(list(parts.values()), 1).astype(np.float32), at


CONST_AT = packed_constants()[1]


class Chain:

    def __init__(self, eng, sem, base=0):
        self.eng, self.sem, self.base, self.n = eng, sem, base, 0

    def add(self, ins):
        self.n += 1
        ins.then_inc(self.sem, 1)

    def wait(self):
        self.eng.wait_ge(self.sem, self.base + self.n)

    def link(self, ins):
        self.add(ins)
        self.wait()


class Carrier:

    def __init__(self, eng, name, met):
        self.eng, self.met = eng, met
        self.kept = eng.alloc_register(name)
        eng.reg_mov(self.kept, 16)

    def wait(self, sem, value):
        self.eng.wait_ge(sem, value)
        if not isinstance(value, int):
            self.eng.reg_alu(self.kept, self.kept, 16, ALU.max)

    def close(self):
        self.eng.wait_ge(self.met, self.eng.snap(self.kept))


def norm_stats(chain, x, stats, mv):
    v = chain.eng
    for t in range(NT):
        chain.add(v.bn_stats(stats[:, t, :], x[:, t, :]))
    chain.wait()
    for t in range(NT):
        ins = v.bn_aggr(mv[:, t, :], stats[:, t, :])
        if t < NT - 1:
            chain.add(ins)
    return ins


def stage_delta(nc, m, A):
    with ExitStack() as ctx:
        sb = lambda n, s, d=F32: ctx.enter_context(nc.sbuf_tensor("d_" + n, s, d))
        sem = lambda n: nc.alloc_semaphore("d_" + n)
        PB = m["PB"]
        C = m["C"]
        xres = m["xres"]
        F, BK = PB[0:2], PB[2:8]

        hT = sb("hT", [P, KD, B * T])
        h = sb("h", [P, NT, D])
        acc = h
        stats = sb("stats", [P, NT, 6])
        mv = sb("mv", [P, NT, 2])
        rstd = sb("rstd", [P, NT])
        wba = sb("wba", [P, KD, 2 * NV])
        convw = sb("convw", [P, NK, 4 * TAPS])
        rows = sb("rows", [P, 2, NV])
        expA = sb("expA", [P, NV])
        normw = sb("normw", [P, 1])
        scal = sb("scal", [P, NK, NSC])
        eyeb = sb("eyeb", [P, P], BF16)
        belowb = sb("belowb", [P, 4, P], BF16)
        W = [sb(f"W{i}", [P, KD, HW]) for i in range(2)]
        wo = [sb(f"wo{i}", [P, RF, D]) for i in range(2)]
        cw = [sb(f"cw{i}", [P, 4 * TAPS]) for i in range(2)]
        hs = [sb(f"hs{i}", [P, NSC]) for i in range(2)]
        kq = [sb(f"kq{i}", [P, NT, 2, P]) for i in range(2)]
        vT = sb("vT", [P, RF, B * T])
        sz = sb("sz", [P, NT, RF * DK])
        cv = [sb(f"cv{i}", [P, 2, T]) for i in range(2)]
        sq = sb("sq", [P, NT, 2, P])
        Gm = sb("Gm", [P, NP, P])
        Dx = sb("Dx", [P, NP, P])
        Vr = Gm
        AP_ = sb("AP", [P, NP, 2, P])
        Abd = sb("Abd", [P, NP, P])
        Am32 = sb("Am32", [P, NP, P])
        TTbd = sb("TTbd", [P, NP, P])
        T64 = sb("T64", [P, NP, P])
        TT = sb("TT", [P, NP, P])
        Tc = sb("Tc", [P, NP, BLK])
        Ttc = sb("Ttc", [P, NP, BLK])
        Yc = sb("Yc", [P, NP, BLK])
        Y2 = sb("Y2", [P, NP, 64])
        t1 = sb("t1", [P, 2 * NT])
        nrm = sb("nrm", [P, 2 * NT])
        rk2 = sb("rk2", [P, NT])
        rq = sb("rq", [P, NT])
        cs = sb("cs", [P, NP])
        kd = sb("kd", [P, NP // 2])
        Kd = sb("Kd", [P, NP // 2, P])
        Wv = sb("Wv", [P, NP, P])
        lin = [Wv[:, 2 * k:2 * k + 2, :].rearrange("p a (b n) -> p (a b) n", n=NV) for k in range(5)]
        S = sb("S", [P, NP // 2, P])
        QSg = Y2[:, :, :].rearrange("p (a b) c -> p a (b c)", b=2)
        szq = Dx
        xg = sb("xg", [P, NP, P])
        ss = sb("ss", [P, NP])
        ss2 = sb("ss2", [P, NP])
        rs = sb("rs", [P, NP])
        yT = AP_[:, 0:NP // 2, :, :].rearrange("p a b c -> p (a b) c")

        names = ["x_in", "const_in", "small_in", "w_in0", "w_in1", "wo_in0", "wo_in1", "lnv", "lnp", "ln_stats", "ln_pow", "h_done",
                 "hT_ps", "hT_done", "zeroed", "bf_const", "ba_done", "beta_done", "actc", "pre_y", "pre_abs", "ln1p", "g_done",
                 "cum_ps", "gam_done", "scal_d", "scal_p", "scal_a", "expA",
                 "proj", "tap0", "tap", "silu", "cwh", "hsc", "gm", "sqd", "logd", "expd", "ssqd", "eps_added", "powd",
                 "csd", "kdd", "rqd", "gram", "apt", "vtp", "vev", "ktp", "kev", "abd_d", "abd_p", "yps", "yev", "xps", "tcd", "ttcd",
                 "exp_d", "exp_a", "t64_d", "t64_p", "t64ps", "ttev", "y2ps", "y2ev", "xtps", "xtev",
                 "w1ps", "w1a", "w1d", "sps", "sa", "sd", "o1ps", "ksps", "r2d", "w2ps", "w2a", "w2d", "qsps", "qsg",
                 "o2ps", "szqd", "xg1", "xg2", "o2add", "ssd", "ss2d", "rsd", "yd", "ytps", "ytev", "ops", "accd", "fin", "finp", "dl"]
        s = {n: sem(n) for n in names}

        def cst(name):
            a, b = CONST_AT[name]
            return C[:, a:b]

        eye, upto, after, ones = cst("eye"), cst("upto"), cst("after"), cst("ones")
        strict, eyepair = cst("strict"), cst("eyec")
        eyec = eyepair[:, 0:BLK]
        levels = cst("levels").rearrange("p (l c) -> p l c", c=BLK)

        x_dram = A["L0_attn_hidden_states"].rearrange("b (c p) d -> p (b c) d", p=P)
        block = ctx.enter_context(nc.Block())
        LAST = NK - 1

        def tl(ti):
            return tile_of(ti // 4, ti % 4)

        YB, XB = (BK[1], BK[3]), (BK[2], BK[4])

        def solved(bank, q=slice(0, P)):
            return bank[q, :].rearrange("p (a j c) -> p a j c", j=4, c=BLK)[:, :, 0:4:3, :]

        def group(x, g, q=slice(0, P)):
            return x[q, 8 * g:8 * g + 8, :].rearrange("p (a j) c -> p a j c", j=2)

        def four(c):
            return c.unsqueeze(1).unsqueeze(1).broadcast_to([c.shape[0], 4, 2, BLK])

        AFTER = {0: "gram", 1: "kt", 2: "y0", 3: "y1", 4: "x1", 5: "y2", 6: "x2", 7: "y3", 8: "x3", 9: "x4", 10: "o2", 11: "o3"}
        SLICES = {}
        for k_, v_ in AFTER.items():
            SLICES.setdefault(v_, []).append(k_)

        @block.sync
        def _(e):
            e.dma_start(xres[:, :, :], x_dram).then_inc(s["x_in"], 16)
            e.dma_start(C[:, :], A["const"]).then_inc(s["const_in"], 16)
            e.dma_start(wba[:, :, :], A["L0_attn_w_ba"].rearrange("(k p) n -> p k n", p=P)).then_inc(s["small_in"], 16)
            e.dma_start(rows[:, 0, :], A["L0_attn_dt_bias"].unsqueeze(0).broadcast_to([P, NV])).then_inc(s["small_in"], 16)
            e.dma_start(rows[:, 1, :], A["L0_attn_A_log"].unsqueeze(0).broadcast_to([P, NV])).then_inc(s["small_in"], 16)
            e.dma_start(convw[:, :, :], A["conv_r"].rearrange("j p n -> p j n")).then_inc(s["small_in"], 16)
            e.dma_start(normw[:, :], A["L0_attn_norm_w"].unsqueeze(1)).then_inc(s["small_in"], 16)
            w_dram = A["L0_attn_w_qkvz"].rearrange("(k p) (j n) -> p j k n", p=P, n=HW)
            wo_dram = A["L0_attn_w_out"].rearrange("(j r p) n -> p j r n", p=P, r=RF)

            def load(n, par, first=False):
                if not first:
                    e.wait_ge(s["proj"], 12 * (n - 1))
                e.dma_start(W[par][:, :, :], w_dram[:, bass.ds(n, 1), :, :].rearrange("p j k n -> p (j k) n")
                            if not isinstance(n, int) else w_dram[:, n, :, :]).then_inc(s[f"w_in{par}"], 16)
                if not first:
                    e.wait_ge(s["ops"], 4 * (n - 1))
                e.dma_start(wo[par][:, :, :], wo_dram[:, bass.ds(n, 1), :, :].rearrange("p j k n -> p (j k) n")
                            if not isinstance(n, int) else wo_dram[:, n, :, :]).then_inc(s[f"wo_in{par}"], 16)

            load(0, 0, True)
            load(1, 1, True)
            with e.Fori(1, NK // 2) as i:
                for par in range(2):
                    load(2 * i + par, par)

        @block.tensor
        def _(e):
            mm, tr = e.matmul, e.transpose
            carrier = Carrier(e, "pe_kept", s["const_in"])

            e.wait_ge(s["const_in"], 16)
            for t in range(NT):
                e.wait_ge(s["h_done"], t + 1)
                for k in range(KD):
                    ins = tr(BK[t // 2][:, (t % 2) * 256 + k * P:(t % 2) * 256 + (k + 1) * P], h[:, t, k * P:(k + 1) * P], eye)
                ins.then_inc(s["hT_ps"], 1)
            e.wait_ge(s["small_in"], 80)
            e.wait_ge(s["hT_done"], 4)
            for t in range(NT):
                for k in range(KD):
                    ins = mm(F[0][:, t * 64:(t + 1) * 64], hT[:, k, t * P:(t + 1) * P], wba[:, k, :], start=(k == 0), stop=(k == KD - 1))
            ins.then_inc(s["ba_done"], 1)
            e.wait_ge(s["g_done"], 1)
            mm(F[1][:, 0:256], upto, lin[1][:, :, :].rearrange("p t n -> p (t n)"), start=True, stop=True)
            mm(F[1][:, 256:512], after, lin[1][:, :, :].rearrange("p t n -> p (t n)"), start=True, stop=True).then_inc(s["cum_ps"], 1)

            def front(n, par, sl):
                if sl == 0:
                    e.wait_ge(s[f"w_in{par}"], 8 * (n - par) + 16)
                if sl >= 2 and sl - 2 < 8:
                    e.wait_ge(s["tap"], 24 * n + 3 * (sl - 2) + 3)
                elif sl >= 2:
                    e.wait_ge(s["silu"], 12 * n + sl - 1)
                elif isinstance(n, int) and n == 0:
                    if sl == 0:
                        e.wait_ge(s["beta_done"], 1)
                        e.wait_ge(s["pre_y"], 2)
                    else:
                        e.wait_ge(s["gam_done"], 2)
                else:
                    e.wait_ge(s["silu"], 12 * n - 1 + sl)
                if sl < 8:
                    col = (1, 0, 2, 3)[sl // 2] * P
                    for k in range(KD):
                        ins = mm(F[sl % 2][:, :], W[par][:, k, col:col + P], hT[:, k, (sl % 2) * 512:(sl % 2 + 1) * 512],
                                 start=(k == 0), stop=(k == KD - 1))
                else:
                    for u in range(2):
                        t = 2 * (sl - 8) + u
                        for k in range(KD):
                            ins = mm(F[sl % 2][:, u * 256:(u + 1) * 256], hT[:, k, t * P:(t + 1) * P], W[par][:, k, 4 * P:6 * P],
                                     start=(k == 0), stop=(k == KD - 1))
                ins.then_inc(s["proj"], 1)

            def body(n, par, with_front):
                def gap(step):
                    if with_front:
                        for sl in SLICES.get(step, ()):
                            front(n + 1, 1 - par, sl)

                kqp, vp = kq[par], vT
                first = isinstance(n, int) and n == 0
                e.wait_ge(s["sqd"], n + 1)
                if not first:
                    e.wait_ge(s["accd"], 4 * n - 3)
                for w in range(2):
                    for t in range(NT):
                        ins = mm(BK[5][:, w * NT + t:w * NT + t + 1], sq[:, t, w, :], ones[:, 0:1], start=True, stop=True)
                ins.then_inc(s["ssqd"], 1)
                for g in range(4):
                    e.wait_ge(s["gm"], NP * n + 4 * g + 4)
                    if not first:
                        e.wait_ge(s["accd"], 4 * n - (2, 1, 0, 0)[g])
                    mm(BK[g][:, :], after, Gm[:, 4 * g:4 * g + 4, :].rearrange("p a b -> p (a b)"), start=True, stop=False)
                    mm(BK[g][:, :], eyeb[:, :], belowb[:, :, :].rearrange("p a b -> p (a b)"), start=False, stop=True).then_inc(s["logd"], 1)
                for g in range(4):
                    if g == 1:
                        e.wait_ge(s["eps_added"], n + 1)
                    if g >= 2:
                        e.wait_ge(s["expd"], 4 * n + g - 1)
                    for u in range(2):
                        t = tl(2 * g + u)
                        ins = mm(BK[(4 + g) % 6][:, u * 256:(u + 1) * 256], kqp[:, t, 0, :], kqp[:, t, :, :].rearrange("p a b -> p (a b)"),
                                 start=True, stop=True)
                    ins.then_inc(s["gram"], 1)
                gap("gram")
                for g in range(4):
                    if g < 2:
                        e.wait_ge(s["expd"], 4 * n + g + 3)
                    else:
                        e.wait_ge(s["apt"], 4 * n + g - 1)
                    for u in range(4):
                        p = 4 * g + u
                        t = tl(p // 2)
                        ins = tr(BK[2 + g][:, u * P:(u + 1) * P], vp[:, p % 2, t * P:(t + 1) * P], eye)
                    ins.then_inc(s["vtp"], 1)
                e.wait_ge(s["apt"], 4 * n + 3)
                for b in range(4):
                    ins = tr(BK[0][:, b * P:(b + 1) * P], kqp[:, tl(b), 0, :], eye)
                ins.then_inc(s["ktp"], 1)
                gap("kt")

                def y_step(r):
                    for g in range(2):
                        if r == 0 and g == 0:
                            e.wait_ge(s["abd_d"], 3 * n + 3)
                            e.wait_ge(s["abd_p"], 3 * n + 1)
                            e.wait_ge(s["apt"], 4 * n + 4)
                        elif r == 0:
                            e.wait_ge(s["vev"], 4 * n + 2)
                        else:
                            e.wait_ge(s["tcd"], 10 * n + 2 * r - 1 + g)
                        if r == 5 and g == 0:
                            e.wait_ge(s["abd_p"], 3 * n + 3)
                        for u in range(8):
                            p = 8 * g + u
                            rhs = eyepair if r == 0 else Tc[:, 2 * (p // 2):2 * (p // 2) + 2, :].rearrange("p a b -> p (a b)")
                            ins = mm(YB[g][:, u * 64:(u + 1) * 64], (Am32 if r == 5 else Abd)[:, p, :], rhs, start=True, stop=True)
                        ins.then_inc(s["yps"], 1)

                def x_step(r):
                    for g in range(2):
                        e.wait_ge(s["yev"], 12 * n + 2 * r + g + 1)
                        if r == 1:
                            e.wait_ge(s["vev"], 4 * n + 1 + 2 * g)
                        e.wait_ge(s["exp_d"], 20 * n + 4 * (r - 1) + 2 * g + 2)
                        e.wait_ge(s["exp_a"], 20 * n + 4 * (r - 1) + 2 * g + 2)
                        for u in range(8):
                            p = 8 * g + u
                            ins = mm(XB[g][:, u * 64:(u + 1) * 64], TTbd[:, p, :],
                                     Yc[:, 2 * (p // 2):2 * (p // 2) + 2, :].rearrange("p a b -> p (a b)"), start=True, stop=True)
                        ins.then_inc(s["xps"], 1)

                y_step(0)
                gap("y0")
                for r in range(1, 6):
                    y_step(r)
                    gap(f"y{r}")
                    x_step(r)
                    gap(f"x{r}")
                e.wait_ge(s["t64_d"], 8 * n + 8)
                e.wait_ge(s["t64_p"], 2 * n + 2)
                e.wait_ge(s["vev"], 4 * n + 4)
                carrier.wait(s["kev"], n + 1)
                for g in range(2):
                    for u in range(8):
                        p = 8 * g + u
                        ins = mm(BK[1 + g][64:128, u * 64:(u + 1) * 64], AP_[0:64, p, 0, 64:128], T64[0:64, p, 0:64], start=True, stop=True)
                    ins.then_inc(s["y2ps"], 1)
                for g in range(4):
                    for u in range(4):
                        p = 4 * g + u
                        ins = tr(BK[(3 + g) % 6][:, u * P:(u + 1) * P], T64[:, p, :], eye)
                    ins.then_inc(s["t64ps"], 1)
                e.wait_ge(s["ttev"], 4 * n + 4)
                for g in range(2):
                    carrier.wait(s["y2ev"], 2 * n + g + 1)
                    for u in range(8):
                        p = 8 * g + u
                        ins = mm(BK[1 + g][0:64, u * 64:(u + 1) * 64], Y2[64:128, p, :], TT[64:128, p, 64:128], start=True, stop=True)
                    ins.then_inc(s["xtps"], 1)

                for g in range(2):
                    e.wait_ge(s["xtev"], 2 * n + g + 1)
                    for u in range(4):
                        p = 4 * g + u
                        ins = mm(BK[3 + g][:, u * P:(u + 1) * P], TT[:, p, :], Vr[:, p, :], start=True, stop=True)
                    ins.then_inc(s["w1ps"], 1)
                for g in range(2):
                    e.wait_ge(s[("w1a", "w1d")[g]], n + 1)
                    for u in range(4):
                        p = 4 * g + u
                        ins = mm(BK[(5 + g) % 6][:, u * P:(u + 1) * P], Kd[:, p, :], Wv[:, p, :], start=True, stop=True)
                    ins.then_inc(s["sps"], 1)
                for g in range(2):
                    for u in range(4):
                        p = 4 * g + u
                        ins = mm(BK[1 + g][:, u * P:(u + 1) * P], AP_[:, p, 1, :], Wv[:, p, :], start=True, stop=True)
                    ins.then_inc(s["o1ps"], 1)
                for g in range(2):
                    e.wait_ge(s[("sa", "sd")[g]], n + 1)
                    for u in range(2):
                        b = 2 * g + u
                        ins = mm(BK[3 + g][:, u * 256:(u + 1) * 256], kqp[:, tl(4 + b), 0, :], S[:, 2 * b:2 * b + 2, :].rearrange("p a b -> p (a b)"),
                                 start=True, stop=True)
                    ins.then_inc(s["ksps"], 1)
                for g in range(2):
                    e.wait_ge(s["r2d"], 2 * n + g + 1)
                    for u in range(4):
                        p = 8 + 4 * g + u
                        ins = mm(BK[(5 + g) % 6][:, u * P:(u + 1) * P], TT[:, p, :], Vr[:, p, :], start=True, stop=True)
                    ins.then_inc(s["w2ps"], 1)
                for g in range(2):
                    for u in range(2):
                        b = 2 * g + u
                        ins = mm(BK[3 + g][:, u * 256:(u + 1) * 256], kqp[:, tl(4 + b), 1, :], S[:, 2 * b:2 * b + 2, :].rearrange("p a b -> p (a b)"),
                                 start=True, stop=True)
                    ins.then_inc(s["qsps"], 1)
                for g in range(2):
                    e.wait_ge(s[("w2a", "w2d")[g]], n + 1)
                    for u in range(4):
                        p = 8 + 4 * g + u
                        ins = mm(BK[(5 + g) % 6][:, u * P:(u + 1) * P], AP_[:, p, 1, :], Wv[:, p, :], start=True, stop=True)
                    ins.then_inc(s["o2ps"], 1)
                def transpose_outputs(g):
                    e.wait_ge(s["yd"], 2 * n + g // 2 + 1)
                    if g < 2:
                        e.wait_ge(s["xg1"], 2 * n + g + 1)
                    else:
                        e.wait_ge(s["qsg"], 2 * n + g - 1)
                    for u in range(4):
                        p = 4 * g + u
                        ins = tr(BK[1 + g][:, u * P:(u + 1) * P], xg[:, p, :], eye)
                    ins.then_inc(s["ytps"], 1)

                def project_outputs(g):
                    e.wait_ge(s["ytev"], 4 * n + g + 1)
                    if g < 2:
                        e.wait_ge(s["xg2"], 2 * n + g + 1)
                    for u in range(2):
                        ti = 2 * g + u
                        for v in range(RF):
                            ins = mm(BK[(5 + g) % 6][:, u * 256:(u + 1) * 256], yT[:, 2 * ti + v, :], wo[par][:, v, :],
                                     start=(v == 0), stop=(v == RF - 1))
                    ins.then_inc(s["ops"], 1)

                transpose_outputs(0)
                transpose_outputs(1)
                gap("o2")
                e.wait_ge(s[f"wo_in{par}"], 8 * (n - par) + 16)
                project_outputs(0)
                project_outputs(1)
                gap("o3")
                transpose_outputs(2)
                transpose_outputs(3)
                project_outputs(2)
                project_outputs(3)

            for sl in range(12):
                front(0, 0, sl)
            body(0, 0, True)
            body(1, 1, True)
            with e.Fori(1, NK // 2 - 1) as i:
                body(2 * i, 0, True)
                body(2 * i + 1, 1, True)
            body(LAST - 1, 0, True)
            body(LAST, 1, False)
            carrier.close()

        @block.scalar
        def _(e):
            ch = Chain(e, s["actc"])
            f = e.activation
            for g in range(4):
                e.wait_ge(s["hT_ps"], 2 * g + 2)
                for u in range(2):
                    ins = f(hT[:, :, (2 * g + u) * P:(2 * g + u + 1) * P],
                            BK[g][:, u * 256:(u + 1) * 256].rearrange("p (k t) -> p k t", k=KD), ACT.Copy)
                ins.then_inc(s["hT_done"], 1)
            ba = F[0][:, :].rearrange("p (t j c) -> p t j c", t=NT, c=2 * RF)
            e.wait_ge(s["ba_done"], 1)
            for t in range(NT):
                ins = f(lin[0][:, t, :].rearrange("p (j v) -> p j v", v=RF), ba[:, t, :, 0:RF], ACT.Sigmoid)
            ins.then_inc(s["beta_done"], 1)
            e.wait_ge(s["pre_y"], 2)
            e.preload_act_table_set("natural_log_exp_and_others")
            ch.link(f(lin[3][:, :, :], lin[2][:, :, :], ACT.Abs))
            ch.link(f(lin[3][:, :, :], lin[3][:, :, :], ACT.Exp, scale=-1.0))
            f(expA[:, :], rows[:, 1, :], ACT.Exp).then_inc(s["expA"], 1)
            f(lin[3][:, :, :], lin[3][:, :, :], ACT.Ln, bias=1.0).then_inc(s["ln1p"], 1)
            e.wait_ge(s["cum_ps"], 1)
            f(lin[2][:, :, :], F[1][:, 0:256].rearrange("p (t n) -> p t n", n=NV), ACT.Exp).then_inc(s["gam_done"], 1)
            f(lin[4][:, :, :], F[1][:, 256:512].rearrange("p (t n) -> p t n", n=NV), ACT.Exp).then_inc(s["gam_done"], 1)
            e.wait_ge(s["gam_done"], 2)
            for k, src in ((GAM, lin[2]), (TAIL, lin[4])):
                for t in range(NT):
                    p0 = (t % 2) * 8 + (t // 2) * 2
                    ins = f(scal[:, :, k + p0:k + p0 + 2], src[:, t, :].rearrange("p (j v) -> p j v", v=RF), ACT.Copy)
                    if k == TAIL and t == NT - 1:
                        ins.then_inc(s["scal_a"], 1)

            def front_tap(n, par, sl):
                if sl == 0:
                    e.wait_ge(s["cwh"], n + 1)
                e.wait_ge(s["proj"], 12 * n + sl + 1)
                if sl < 8:
                    if sl >= 2:
                        e.wait_ge(s["silu"], 12 * n + sl - 1)
                    elif not (isinstance(n, int) and n == 0):
                        e.wait_ge(s["silu"], 12 * n - 4)
                    w = (1, 0, 2, 3)[sl // 2] * TAPS + TAPS - 1
                    f(cv[sl % 2][:, :, :], F[sl % 2][:, :].rearrange("p (b t) -> p b t", b=2), ACT.Copy,
                      scale=cw[par][:, w:w + 1]).then_inc(s["tap0"], 1)
                else:
                    if sl == 8 and not (isinstance(n, int) and n == 0):
                        e.wait_ge(s["szqd"], 8 * n)
                    f(sz[:, 2 * (sl - 8):2 * (sl - 8) + 2, :], F[sl % 2][:, :].rearrange("p (t c) -> p t c", t=2), ACT.Silu)\
                        .then_inc(s["silu"], 1)

            def front_silu(n, par, sl):
                e.wait_ge(s["tap"], 24 * n + 3 * sl + 3)
                half, which = sl % 2, sl // 2
                src = cv[sl % 2][:, :, :].rearrange("p b t -> p (b t)")
                if which < 2:
                    dst = kq[par][:, 4 * half:4 * half + 4, which, :]
                    src = src.rearrange("p (t c) -> p t c", c=P)
                else:
                    dst = vT[:, which - 2, 512 * half:512 * half + 512]
                f(dst, src, ACT.Silu).then_inc(s["silu"], 1)

            def front(n, par, sl):
                front_tap(n, par, sl) if sl < 8 else None
                if 1 <= sl <= 8:
                    front_silu(n, par, sl - 1)
                if sl >= 8:
                    front_tap(n, par, sl)

            def body(n, par, with_front):
                def gap(step):
                    if with_front:
                        for sl in SLICES.get(step, ()):
                            front(n + 1, 1 - par, sl)

                def expand(r):
                    for g in range(2):
                        e.wait_ge(s["ttcd"], 10 * n + 2 * r + g + 1)
                        for i in (1, 2):
                            q = slice(32 * i, 32 * i + 32)
                            f(TTbd[q, 8 * g:8 * g + 8, q], Ttc[q, 8 * g:8 * g + 8, :], ACT.Copy).then_inc(s["exp_a"], 1)

                for g in range(4):
                    e.wait_ge(s["logd"], 4 * n + g + 1)
                    if not (isinstance(n, int) and n == 0):
                        e.wait_ge(s["xg2"], 2 * n)
                    f(Dx[:, 4 * g:4 * g + 4, :], BK[g][:, :].rearrange("p (a b) -> p a b", a=4), ACT.Exp).then_inc(s["expd"], 1)
                gap("gram")
                e.wait_ge(s["powd"], n + 1)
                for g in range(4):
                    e.wait_ge(s["vtp"], 4 * n + g + 1)
                    for u in range(2):
                        p = 4 * g + 2 * u
                        t = tl(p // 2)
                        ins = f(Vr[:, p:p + 2, :], BK[2 + g][:, u * 256:(u + 1) * 256].rearrange("p (a b) -> p a b", a=2), ACT.Copy,
                                scale=nrm[:, t:t + 1])
                    ins.then_inc(s["vev"], 1)
                gap("kt")
                expand(0)
                gap("y0")
                for r in range(1, 6):
                    gap(f"y{r}")
                    if r < 5:
                        expand(r)
                    gap(f"x{r}")
                for g in range(4):
                    e.wait_ge(s["t64ps"], 4 * n + g + 1)
                    f(TT[:, 4 * g:4 * g + 4, :], BK[(3 + g) % 6][:, :].rearrange("p (a b) -> p a b", a=4), ACT.Copy).then_inc(s["ttev"], 1)
                e.wait_ge(s["w1ps"], 2 * n + 1)
                f(Wv[:, 0:4, :], BK[3][:, :].rearrange("p (a b) -> p a b", a=4), ACT.Copy).then_inc(s["w1a"], 1)
                e.wait_ge(s["sps"], 2 * n + 1)
                f(S[:, 0:4, :], BK[5][:, :].rearrange("p (a b) -> p a b", a=4), ACT.Copy).then_inc(s["sa"], 1)

                def squares(c):
                    if c:
                        e.wait_ge(s["ssd"], 2 * n + 1)
                    for p in range(8 * c, 8 * c + 8):
                        ins = f(Kd[:, p % 8, :], xg[:, p, :], ACT.Square, accum_out=ss[:, p:p + 1])
                    ins.then_inc(s["ssd"], 1)

                e.wait_ge(s["xg1"], 2 * n + 2)
                squares(0)
                e.wait_ge(s["w2ps"], 2 * n + 1)
                f(Wv[:, 8:12, :], BK[5][:, :].rearrange("p (a b) -> p a b", a=4), ACT.Copy).then_inc(s["w2a"], 1)
                for g in range(2):
                    e.wait_ge(s["qsps"], 2 * n + g + 1)
                    for u in range(4):
                        q = 4 * g + u
                        ins = f(QSg[:, q, :], BK[3 + g][:, u * P:(u + 1) * P], ACT.Copy, scale=hs[par][:, GAM + 8 + q:GAM + 9 + q])
                    ins.then_inc(s["qsg"], 1)

                def outputs(g):
                    e.wait_ge(s["ytps"], 4 * n + g + 1)
                    f(yT[:, 4 * g:4 * g + 4, :], BK[1 + g][:, :].rearrange("p (a b) -> p a b", a=4), ACT.Copy, scale=normw[:, 0:1])\
                        .then_inc(s["ytev"], 1)

                outputs(0)
                outputs(1)
                e.wait_ge(s["xg2"], 2 * n + 2)
                squares(1)
                gap("o2")
                gap("o3")
                outputs(2)
                outputs(3)

            for sl in range(12):
                front(0, 0, sl)
            body(0, 0, True)
            body(1, 1, True)
            with e.Fori(1, NK // 2 - 1) as i:
                body(2 * i, 0, True)
                body(2 * i + 1, 1, True)
            body(LAST - 1, 0, True)
            body(LAST, 1, False)

        @block.vector
        def _(e):
            tt, ts, stt = e.tensor_tensor, e.tensor_scalar, e.scalar_tensor_tensor
            ch = Chain(e, s["lnv"])
            e.memset(Abd[:, :, :], 0.0).then_inc(s["zeroed"], 1)
            e.memset(TTbd[:, :, :], 0.0).then_inc(s["zeroed"], 1)
            e.wait_ge(s["x_in"], 16)
            norm_stats(ch, xres, stats, mv).then_inc(s["ln_stats"], 1)
            e.wait_ge(s["ln_pow"], 1)
            for t in range(NT):
                ts(h[:, t, :], xres[:, t, :], mv[:, t, 0:1], rstd[:, t:t + 1], ALU.subtract, ALU.mult).then_inc(s["h_done"], 1)
            e.wait_ge(s["const_in"], 16)
            e.tensor_copy(eyeb[:, :], eye).then_inc(s["bf_const"], 1)
            e.tensor_copy(belowb[:, :, :], over(cst("below"), 4)).then_inc(s["bf_const"], 1)
            e.wait_ge(s["small_in"], 80)
            e.wait_ge(s["beta_done"], 1)
            ba = F[0][:, :].rearrange("p (t j c) -> p t j c", t=NT, c=2 * RF)
            for t in range(NT):
                ins = tt(lin[2][:, t, :].rearrange("p (j v) -> p j v", v=RF), ba[:, t, :, RF:2 * RF],
                         rows[:, 0, :].rearrange("p (j v) -> p j v", v=RF), ALU.add)
            ins.then_inc(s["pre_y"], 1)
            e.wait_ge(s["pre_y"], 1)
            ts(lin[1][:, :, :], lin[2][:, :, :], 0.0, None, ALU.max).then_inc(s["pre_y"], 1)
            e.wait_ge(s["ln1p"], 1)
            e.wait_ge(s["pre_y"], 2)
            ch.link(tt(lin[1][:, :, :], lin[1][:, :, :], lin[3][:, :, :], ALU.add))
            e.wait_ge(s["expA"], 1)
            stt(out=lin[1][:, :, :], in0=lin[1][:, :, :], scalar=-1.0, in1=over(expA[:, :], NT), op0=ALU.mult, op1=ALU.mult)\
                .then_inc(s["g_done"], 1)
            e.wait_ge(s["gam_done"], 2)
            ch.link(ts(lin[3][:, :, :], lin[2][:, :, :], -1.0, None, ALU.mult))
            for t in range(NT):
                p0 = (t % 2) * 8 + (t // 2) * 2
                ins = e.tensor_copy(scal[:, :, NEGGAM + p0:NEGGAM + p0 + 2], lin[3][:, t, :].rearrange("p (j v) -> p j v", v=RF))
            ins.then_inc(s["scal_d"], 1)

            def front(n, par, sl):
                if sl >= 8:
                    return
                e.wait_ge(s["tap0"], 8 * n + sl + 1)
                x = F[sl % 2][:, :].rearrange("p (b t) -> p b t", b=2)
                w0 = (1, 0, 2, 3)[sl // 2] * TAPS
                for k in range(1, TAPS):
                    if k > 1:
                        e.wait_ge(s["tap"], 24 * n + 3 * sl + k - 1)
                    o = cv[sl % 2][:, :, k:T]
                    stt(out=o, in0=x[:, :, 0:T - k], scalar=cw[par][:, w0 + TAPS - 1 - k:w0 + TAPS - k], in1=o,
                        op0=ALU.mult, op1=ALU.add).then_inc(s["tap"], 1)

            DL = 3

            def body(n, par, with_front):
                def gap(step):
                    if with_front:
                        for sl in SLICES.get(step, ()):
                            front(n + 1, 1 - par, sl)

                dl = Chain(e, s["dl"], base=DL * n)
                h_ = hs[par]
                e.wait_ge(s["ssqd"], n + 1)
                ts(t1[:, :], BK[5][:, 0:2 * NT], 1e-6, None, ALU.add).then_inc(s["eps_added"], 1)
                e.wait_ge(s["eps_added"], n + 1)
                dl.link(e.reciprocal(rk2[:, :], t1[:, 0:NT]))
                e.wait_ge(s["hsc"], n + 1)
                dl.link(tt(cs[:, :].rearrange("p (c b v) -> p c b v", c=2, b=4), h_[:, BETA:BETA + NP].rearrange("p (c b v) -> p c b v", c=2, b=4),
                           rk2[:, :].rearrange("p (b c) -> p c b", c=2).unsqueeze(3).broadcast_to([P, 2, 4, 2]), ALU.mult))
                dl.add(tt(kd[:, :], cs[:, 0:8], h_[:, TAIL:TAIL + 8], ALU.mult))
                for g in range(4):
                    e.wait_ge(s["gram"], 4 * n + g + 1)
                    e.wait_ge(s["expd"], 4 * n + g + 1)
                    for u in range(4):
                        p = 4 * g + u
                        ins = stt(out=AP_[:, p, :, :], in0=Dx[:, p, :].unsqueeze(1).broadcast_to([P, 2, P]), scalar=cs[:, p:p + 1],
                                  in1=BK[(4 + g) % 6][:, (u // 2) * 256:(u // 2 + 1) * 256].rearrange("p (a b) -> p a b", a=2),
                                  op0=ALU.mult, op1=ALU.mult)
                    ins.then_inc(s["apt"], 1)
                e.wait_ge(s["apt"], 4 * n + 4)
                for i in range(3):
                    q = slice(32 * i, 32 * i + 32)
                    tt(Abd[q, :, q], AP_[q, :, 0, q], over(strict[q, :], NP), ALU.mult).then_inc(s["abd_d"], 1)
                e.wait_ge(s["powd"], n + 1)
                ts(rq[:, :], nrm[:, NT:2 * NT], DK ** -0.5, None, ALU.mult).then_inc(s["rqd"], 1)
                gap("gram")
                gap("kt")
                for r in range(5):
                    for g in range(2):
                        e.wait_ge(s["yps"], 12 * n + 2 * r + g + 1)
                        tt(group(Yc, g), solved(YB[g]), four(levels[:, r, :]), ALU.mult).then_inc(s["yev"], 1)
                    if r:
                        gap(f"y{r}")
                    for g in range(2):
                        gs = slice(8 * g, 8 * g + 8)
                        if r:
                            e.wait_ge(s["xps"], 10 * n + 2 * r - 1 + g)
                            tt(group(Tc, g), group(Tc, g), solved(XB[g]), ALU.subtract).then_inc(s["tcd"], 1)
                        else:
                            e.wait_ge(s["yev"], 12 * n + 1 + g)
                            tt(Tc[:, gs, :], over(eyec, 8), Yc[:, gs, :], ALU.subtract).then_inc(s["tcd"], 1)
                        e.wait_ge(s["tcd"], 10 * n + 2 * r + g + 1)
                        if r:
                            e.wait_ge(s["exp_a"], 20 * n + 4 * (r - 1) + 2 * g + 2)
                        e.transpose(Ttc[:, gs, :].rearrange("p a b -> p (a b)"), Tc[:, gs, :].rearrange("p a b -> p (a b)")).then_inc(s["ttcd"], 1)
                        e.wait_ge(s["ttcd"], 10 * n + 2 * r + g + 1)
                        for i in (0, 3):
                            q = slice(32 * i, 32 * i + 32)
                            e.tensor_copy(TTbd[q, gs, q], Ttc[q, gs, :]).then_inc(s["exp_d"], 1)
                    gap(f"x{r}" if r else "y0")
                dl.wait()
                e.wait_ge(s["ktp"], n + 1)
                for p in range(8):
                    ins = ts(Kd[:, p, :], BK[0][:, (p // 2) * P:(p // 2 + 1) * P], kd[:, p:p + 1], None, ALU.mult)
                ins.then_inc(s["kev"], 1)
                for g in range(2):
                    e.wait_ge(s["yps"], 12 * n + 11 + g)
                    e.tensor_copy(group(Yc, g), solved(YB[g])).then_inc(s["yev"], 1)
                gap("y5")
                ev = cst("even")
                for g in range(2):
                    e.wait_ge(s["xps"], 10 * n + 9 + g)
                    for hf in range(2):
                        q = slice(64 * hf, 64 * hf + 64)
                        for j in range(2):
                            ps = slice(8 * g + j, 8 * g + 8, 2)
                            stt(out=T64[q, ps, 64 * hf:64 * hf + 32], in0=Tc[q, ps, :], scalar=ev[q, :], in1=solved(XB[g], q)[:, :, j, :],
                                op0=ALU.mult, op1=ALU.subtract).then_inc(s["t64_d"], 1)
                gap("x5")
                for g in range(2):
                    e.wait_ge(s["y2ps"], 2 * n + g + 1)
                    e.tensor_copy(Y2[64:128, 8 * g:8 * g + 8, :], BK[1 + g][64:128, :].rearrange("p (a b) -> p a b", a=8)).then_inc(s["y2ev"], 1)
                for g in range(2):
                    e.wait_ge(s["xtps"], 2 * n + g + 1)
                    ts(TT[0:64, 8 * g:8 * g + 8, 64:128], BK[1 + g][0:64, :].rearrange("p (a b) -> p a b", a=8), -1.0, None, ALU.mult)\
                        .then_inc(s["xtev"], 1)
                e.wait_ge(s["w1ps"], 2 * n + 2)
                e.tensor_copy(Wv[:, 4:8, :], BK[4][:, :].rearrange("p (a b) -> p a b", a=4)).then_inc(s["w1d"], 1)
                e.wait_ge(s["sps"], 2 * n + 2)
                e.tensor_copy(S[:, 4:8, :], BK[0][:, :].rearrange("p (a b) -> p a b", a=4)).then_inc(s["sd"], 1)
                e.wait_ge(s["szqd"], 8 * n + 8)
                for g in range(2):
                    e.wait_ge(s["o1ps"], 2 * n + g + 1)
                    tt(xg[:, 4 * g:4 * g + 4, :], BK[1 + g][:, :].rearrange("p (a b) -> p a b", a=4), szq[:, 4 * g:4 * g + 4, :], ALU.mult)\
                        .then_inc(s["xg1"], 1)
                for g in range(2):
                    e.wait_ge(s["ksps"], 2 * n + g + 1)
                    for u in range(4):
                        p = 8 + 4 * g + u
                        ins = stt(out=Vr[:, p, :], in0=BK[3 + g][:, u * P:(u + 1) * P], scalar=h_[:, NEGGAM + p:NEGGAM + p + 1], in1=Vr[:, p, :],
                                  op0=ALU.mult, op1=ALU.add)
                    ins.then_inc(s["r2d"], 1)

                def scale_rows(c):
                    e.wait_ge(s["ssd"], 2 * n + c + 1)
                    q = slice(8 * c, 8 * c + 8)
                    ts(ss2[:, q], ss[:, q], 1.0 / DK, 1e-6, ALU.mult, ALU.add).then_inc(s["ss2d"], 1)

                def apply_rows(c):
                    e.wait_ge(s["rsd"], 2 * n + c + 1)
                    for p in range(8 * c, 8 * c + 8):
                        ins = ts(xg[:, p, :], xg[:, p, :], rs[:, p:p + 1], None, ALU.mult)
                    ins.then_inc(s["yd"], 1)

                scale_rows(0)
                e.wait_ge(s["w2ps"], 2 * n + 2)
                e.tensor_copy(Wv[:, 12:16, :], BK[0][:, :].rearrange("p (a b) -> p a b", a=4)).then_inc(s["w2d"], 1)
                apply_rows(0)
                for g in range(2):
                    e.wait_ge(s["o2ps"], 2 * n + g + 1)
                    e.wait_ge(s["qsg"], 2 * n + g + 1)
                    tt(QSg[:, 4 * g:4 * g + 4, :], BK[(5 + g) % 6][:, :].rearrange("p (a b) -> p a b", a=4), QSg[:, 4 * g:4 * g + 4, :], ALU.add)\
                        .then_inc(s["o2add"], 1)
                    e.wait_ge(s["o2add"], 2 * n + g + 1)
                    tt(xg[:, 8 + 4 * g:12 + 4 * g, :], QSg[:, 4 * g:4 * g + 4, :], szq[:, 8 + 4 * g:12 + 4 * g, :], ALU.mult).then_inc(s["xg2"], 1)
                scale_rows(1)
                apply_rows(1)
                gap("o2")
                gap("o3")
                for g in range(4):
                    e.wait_ge(s["ops"], 4 * n + g + 1)
                    c, b0 = g // 2, 2 * (g % 2)
                    dst = acc[:, :, :].rearrange("p (b c) d -> p c b d", c=2)[:, c, b0:b0 + 2, :]
                    src = BK[(5 + g) % 6][:, :].rearrange("p (a b) -> p a b", a=2)
                    if isinstance(n, int) and n == 0:
                        e.tensor_copy(dst, src).then_inc(s["accd"], 1)
                    else:
                        tt(dst, dst, src, ALU.add).then_inc(s["accd"], 1)
                assert dl.n == DL

            for sl in range(12):
                front(0, 0, sl)
            body(0, 0, True)
            body(1, 1, True)
            with e.Fori(1, NK // 2 - 1) as i:
                body(2 * i, 0, True)
                body(2 * i + 1, 1, True)
            body(LAST - 1, 0, True)
            body(LAST, 1, False)

            e.wait_ge(s["accd"], 4 * NK)
            norm_stats(ch, acc, stats, mv).then_inc(s["ln_stats"], 1)
            e.wait_ge(s["ln_pow"], 2)
            for t in range(NT):
                ch.add(ts(acc[:, t, :], acc[:, t, :], mv[:, t, 0:1], rstd[:, t:t + 1], ALU.subtract, ALU.mult))
            ch.wait()
            for t in range(NT):
                tt(xres[:, t, :], xres[:, t, :], acc[:, t, :], ALU.add).then_inc(s["fin"], 1)
            e.wait_ge(s["fin"], NT)

        @block.gpsimd
        def _(e):
            tt, ts = e.tensor_tensor, e.tensor_scalar
            ch = Chain(e, s["lnp"])
            e.memset(Am32[:, :, :], 0.0).then_inc(s["zeroed"], 1)
            e.memset(T64[:, :, :], 0.0).then_inc(s["zeroed"], 1)

            def rstd_of(k):
                e.wait_ge(s["ln_stats"], k)
                ch.link(ts(rstd[:, :], mv[:, :, 1], LN_EPS, None, ALU.add))
                e.tensor_tensor(rstd[:, :], rstd[:, :], cst("mhalf")[:, 0:NT], ALU.pow).then_inc(s["ln_pow"], 1)

            e.wait_ge(s["const_in"], 16)
            rstd_of(1)
            for k, src, w in ((BETA, lin[0], "beta_done"), (LOGDECAY, lin[1], "g_done")):
                e.wait_ge(s[w], 1)
                for t in range(NT):
                    p0 = (t % 2) * 8 + (t // 2) * 2
                    ins = e.tensor_copy(scal[:, :, k + p0:k + p0 + 2], src[:, t, :].rearrange("p (j v) -> p j v", v=RF))
            ins.then_inc(s["scal_p"], 1)
            e.wait_ge(s["scal_p"], 1)
            e.wait_ge(s["scal_d"], 1)
            e.wait_ge(s["scal_a"], 1)

            carrier = Carrier(e, "pool_kept", s["const_in"])
            wait = carrier.wait

            def front_scalars(n, par):
                if isinstance(n, int):
                    cs_, ss_ = convw[:, n, :], scal[:, n, :]
                else:
                    cs_ = convw[:, bass.ds(n, 1), :].rearrange("p a b -> p (a b)")
                    ss_ = scal[:, bass.ds(n, 1), :].rearrange("p a b -> p (a b)")
                if not (isinstance(n, int) and n < 2):
                    wait(s["tap"], 24 * (n - 1))
                    wait(s["r2d"], 2 * (n - 1))
                    wait(s["qsg"], 2 * (n - 1))
                e.tensor_copy(cw[par][:, :], cs_).then_inc(s["cwh"], 1)
                e.tensor_copy(hs[par][:, :], ss_).then_inc(s["hsc"], 1)

            def front_decays(n, par):
                wait(s["hsc"], n + 1)
                if not (isinstance(n, int) and n == 0):
                    wait(s["w2ps"], 2 * n)
                for p in range(NP):
                    ts(Gm[:, p, :], upto, hs[par][:, LOGDECAY + p:LOGDECAY + p + 1], 1.0, ALU.mult, ALU.mult).then_inc(s["gm"], 1)

            def front_squares(n, par):
                wait(s["silu"], 12 * n + 4)
                if not (isinstance(n, int) and n == 0):
                    wait(s["ssqd"], n)
                tt(sq[:, :, :, :], kq[par][:, :, :, :], kq[par][:, :, :, :], ALU.mult).then_inc(s["sqd"], 1)

            def body(n, par, with_front):
                if with_front:
                    front_scalars(n + 1, 1 - par)
                wait(s["eps_added"], n + 1)
                tt(nrm[:, :], t1[:, :], cst("pows"), ALU.pow).then_inc(s["powd"], 1)
                wait(s["apt"], 4 * n + 4)
                wait(s["powd"], n + 1)
                if not (isinstance(n, int) and n == 0):
                    wait(s["yps"], 12 * n)
                tt(Abd[96:128, :, 96:128], AP_[96:128, :, 0, 96:128], over(strict[96:128, :], NP), ALU.mult).then_inc(s["abd_p"], 1)
                wait(s["abd_p"], 3 * n + 1)
                e.tensor_copy(Am32[0:32, :, 32:64], AP_[0:32, :, 0, 32:64]).then_inc(s["abd_p"], 1)
                wait(s["abd_p"], 3 * n + 2)
                e.tensor_copy(Am32[64:96, :, 96:128], AP_[64:96, :, 0, 96:128]).then_inc(s["abd_p"], 1)
                wait(s["abd_p"], 3 * n + 3)
                wait(s["rqd"], n + 1)
                for ti in range(NT):
                    t = tl(ti)
                    ts(szq[:, 2 * ti:2 * ti + 2, :].rearrange("p a b -> p (a b)"), sz[:, t, :], rq[:, t:t + 1], 1.0, ALU.mult, ALU.mult)\
                        .then_inc(s["szqd"], 1)
                wait(s["szqd"], 8 * n + 8)
                if with_front:
                    front_squares(n + 1, 1 - par)
                wait(s["tcd"], 10 * n + 10)
                if not (isinstance(n, int) and n == 0):
                    wait(s["t64ps"], 4 * n)
                od = cst("odd")
                for hf in range(2):
                    q = slice(64 * hf, 64 * hf + 64)
                    ts(T64[q, :, 64 * hf + 32:64 * hf + 64], Tc[q, :, :], od[q, :], 1.0, ALU.mult, ALU.mult).then_inc(s["t64_p"], 1)
                    wait(s["t64_p"], 2 * n + hf + 1)

                def rsqrt_rows(c):
                    wait(s["ss2d"], 2 * n + c + 1)
                    q = slice(8 * c, 8 * c + 8)
                    tt(rs[:, q], ss2[:, q], cst("mhalf")[:, q], ALU.pow).then_inc(s["rsd"], 1)

                rsqrt_rows(0)
                if with_front:
                    front_decays(n + 1, 1 - par)
                rsqrt_rows(1)

            front_scalars(0, 0)
            front_decays(0, 0)
            front_squares(0, 0)
            body(0, 0, True)
            body(1, 1, True)
            with e.Fori(1, NK // 2 - 1) as i:
                body(2 * i, 0, True)
                body(2 * i + 1, 1, True)
            body(LAST - 1, 0, True)
            body(LAST, 1, False)
            rstd_of(2)
            carrier.close()


def over(ap, n):
    return ap.unsqueeze(1).broadcast_to([ap.shape[0], n, ap.shape[1]])


def along(ap, n):
    return ap.unsqueeze(2).broadcast_to([ap.shape[0], ap.shape[1], n])


class RowNorm:

    def __init__(self, ctx, nc, prefix, mhalf):
        self.stats = ctx.enter_context(nc.sbuf_tensor(prefix + "stats", [P, NT, 6], F32))
        self.mv = ctx.enter_context(nc.sbuf_tensor(prefix + "mv", [P, NT, 2], F32))
        self.rstd = ctx.enter_context(nc.sbuf_tensor(prefix + "rstd", [P, NT], F32))
        self.moments = nc.alloc_semaphore(prefix + "moments")
        self.rooted = nc.alloc_semaphore(prefix + "rooted")
        self.mhalf = mhalf

    def vector(self, ch, src, dst, k, done):
        v = ch.eng
        norm_stats(ch, src, self.stats, self.mv).then_inc(self.moments, 1)
        v.wait_ge(self.rooted, k)
        for t in range(NT):
            v.tensor_scalar(dst[:, t, :], src[:, t, :], self.mv[:, t, 0:1], self.rstd[:, t:t + 1],
                            ALU.subtract, ALU.mult).then_inc(done, 1)

    def pool(self, ch, k):
        g = ch.eng
        g.wait_ge(self.moments, k)
        ch.link(g.tensor_scalar(self.rstd[:, :], self.mv[:, :, 1], LN_EPS, None, ALU.add))
        g.tensor_tensor(self.rstd[:, :], self.rstd[:, :], self.mhalf[:, 0:NT], ALU.pow).then_inc(self.rooted, 1)


NS = B * TOP
NH, NKV, HD = 16, 8, 128
QKV = (NH + 2 * NKV) * HD
FF = 1024
RMS_EPS = 1e-6
ROPE_THETA = 10000.0


def stage_top(nc, m, A):
    assert NS == P
    with ExitStack() as ctx:
        sb = lambda n, s, d=F32: ctx.enter_context(nc.sbuf_tensor("t_" + n, s, d))
        sem = lambda n: nc.alloc_semaphore("t_" + n)
        PB, C, xres = m["PB"], m["C"], m["xres"]

        def cst(name):
            a, b = CONST_AT[name]
            return C[:, a:b]

        eye = cst("eye")
        ln = RowNorm(ctx, nc, "t_", cst("mhalf"))
        h = sb("h", [P, NT, D])
        wr = sb("wr", [P, D])
        lnw = sb("lnw", [P, 2, D])
        bias = sb("bias", [P, QKV])
        wqkv = sb("wqkv", [P, KD, QKV])
        wo = sb("wo", [P, NH, D])
        wgu = sb("wgu", [P, KD, 2 * FF])
        wd = sb("wd", [P, FF // P, D])
        rope = sb("rope", [P, 2, 2 * HD])
        prod = sb("prod", [P, NT, D])
        sc = sb("sc", [P, NT])
        row = sb("row", [B, T])
        work = [sb(f"work{i}", [B, T]) for i in range(2)]
        top8 = sb("top8", [B, TOP])
        mask = sb("mask", [B, T])
        pos = sb("pos", [B, T])
        slot = sb("slot", [P, NT])
        E_ = sb("E", [P, NT, P])
        ET = sb("ET", [P, NT, P])
        xs = sb("xs", [P, D])
        cossin = sb("cossin", [P, 2, HD])
        sq = sb("sq", [P, D])
        ms = sb("ms", [P, 4])
        hh = sb("hh", [P, D])
        hT = sb("hT", [P, KD, P])
        qkv = sb("qkv", [P, NH + 2 * NKV, HD])
        rot = sb("rot", [P, NH + NKV, HD])
        qkT = sb("qkT", [P, NH + NKV, P])
        att = sb("att", [P, NH, P])
        attT = rot[:, 0:NH, :]
        oT = sb("oT", [P, NH, P])
        mx = sb("mx", [P, NH])
        sm = sb("sm", [P, NH])
        x1 = sb("x1", [P, D])
        mid = qkv[:, 0:FF // HD, :].rearrange("p a b -> p (a b)")
        midT = sb("midT", [P, FF // P, P])
        gate = sb("gate", [P, 1])
        ones_b = cst("ones")

        names = ["in_a", "in_qkv", "in_wo", "in_gu", "in_d", "v", "a", "g", "h", "sc", "rowT", "code", "slotT", "E", "gathered",
                 "xs", "ss", "rms", "hh", "hTp", "hT", "qkvp", "qkv", "rope_g", "rope", "trp", "tre", "sp", "att", "mx", "exp", "nrm",
                 "pTp", "pT", "op", "oT", "wop", "x1", "gup", "silu", "mid", "mTp", "mT", "dp", "delta", "ETp", "ET", "scp", "out", "gate", "ln2", "fin"]
        s = {n: sem(n) for n in names}
        block = ctx.enter_context(nc.Block())

        def bank4(i):
            return PB[i][:, :].rearrange("p (a b) -> p a b", b=P)

        @block.sync
        def _(e):
            row_of = lambda name, n: A[name].unsqueeze(0).broadcast_to([P, n])
            e.dma_start(wr[:, :], row_of("L0_ffn_w_router", D)).then_inc(s["in_a"], 16)
            e.dma_start(lnw[:, 0, :], row_of("L0_ffn_ln1_w", D)).then_inc(s["in_a"], 16)
            e.dma_start(lnw[:, 1, :], row_of("L0_ffn_ln2_w", D)).then_inc(s["in_a"], 16)
            e.dma_start(rope[:, :, :], A["rope"].rearrange("(c p) n -> p c n", p=P)).then_inc(s["in_a"], 16)
            at = 0
            for name, bname, n in (("L0_ffn_wq", "L0_ffn_bq", NH), ("L0_ffn_wk", "L0_ffn_bk", NKV), ("L0_ffn_wv", "L0_ffn_bv", NKV)):
                e.dma_start(wqkv[:, :, at:at + n * HD], A[name].rearrange("(k p) n -> p k n", p=P)).then_inc(s["in_qkv"], 16)
                e.dma_start(bias[:, at:at + n * HD], row_of(bname, n * HD)).then_inc(s["in_qkv"], 16)
                at += n * HD
            e.dma_start(wo[:, :, :], A["L0_ffn_wo"].rearrange("(h p) n -> p h n", p=P)).then_inc(s["in_wo"], 16)
            e.dma_start(wgu[:, :, 0:FF], A["L0_ffn_w_gate"].rearrange("(k p) n -> p k n", p=P)).then_inc(s["in_gu"], 16)
            e.dma_start(wgu[:, :, FF:2 * FF], A["L0_ffn_w_up"].rearrange("(k p) n -> p k n", p=P)).then_inc(s["in_gu"], 16)
            e.dma_start(wd[:, :, :], A["L0_ffn_w_down"].rearrange("(k p) n -> p k n", p=P)).then_inc(s["in_d"], 16)

        @block.tensor
        def _(e):
            mm, tr = e.matmul, e.transpose
            e.wait_ge(s["sc"], 1)
            for c in range(2):
                ins = tr(PB[0][0:B, c * P:(c + 1) * P], sc[:, c::2], eye)
            ins.then_inc(s["rowT"], 1)
            e.wait_ge(s["code"], 1)
            for c in range(2):
                ins = tr(PB[1][:, c * B:(c + 1) * B], pos[:, c * P:(c + 1) * P], eye[0:B, 0:B])
            ins.then_inc(s["slotT"], 1)
            e.wait_ge(s["E"], NT)
            for t in range(NT):
                mm(PB[2][:, 0:D], E_[:, t, :], h[:, t, :], start=(t == 0), stop=(t == NT - 1))
            e.wait_ge(s["in_a"], 64)
            for t in range(NT):
                ins = mm(PB[3][:, 0:2 * HD], E_[:, t, :], rope[:, t % 2, :], start=(t == 0), stop=(t == NT - 1))
            ins.then_inc(s["gathered"], 1)
            for g in range(2):
                for u in range(4):
                    ins = tr(PB[g][:, u * P:(u + 1) * P], E_[:, 4 * g + u, :], eye)
                ins.then_inc(s["ETp"], 1)

            def turn_rows(k):
                e.wait_ge(s["hh"], k)
                for j in range(KD):
                    ins = tr(PB[7][:, j * P:(j + 1) * P], hh[:, j * P:(j + 1) * P], eye)
                ins.then_inc(s["hTp"], 1)
                e.wait_ge(s["hT"], k)

            turn_rows(1)
            e.wait_ge(s["in_qkv"], 96)
            e.wait_ge(s["xs"], 2)
            e.wait_ge(s["ET"], 2)
            for g in range(8):
                for k in range(KD):
                    ins = mm(PB[g][:, :], hT[:, k, :], wqkv[:, k, g * 512:(g + 1) * 512], start=(k == 0), stop=(k == KD - 1))
                ins.then_inc(s["qkvp"], 1)
            e.wait_ge(s["qkv"], 8)
            for g in range(6):
                e.wait_ge(s["rope"], 1 if g < 4 else 2)
                for u in range(4):
                    ins = tr(PB[g][:, u * P:(u + 1) * P], qkv[:, 4 * g + u, :], eye)
                ins.then_inc(s["trp"], 1)
            e.wait_ge(s["tre"], 6)
            for g in range(4):
                for u in range(4):
                    hd = 4 * g + u
                    ins = mm(PB[g][:, u * P:(u + 1) * P], qkT[:, hd, :], qkT[:, NH + hd // 2, :], start=True, stop=True)
                ins.then_inc(s["sp"], 1)
            for g in range(4):
                e.wait_ge(s["nrm"], 4 * g + 4)
                for u in range(4):
                    ins = tr(PB[4 + g][:, u * P:(u + 1) * P], att[:, 4 * g + u, :], eye)
                ins.then_inc(s["pTp"], 1)
            for g in range(4):
                e.wait_ge(s["pT"], g + 1)
                for u in range(4):
                    hd = 4 * g + u
                    ins = mm(PB[g][:, u * P:(u + 1) * P], qkv[:, NH + NKV + hd // 2, :], attT[:, hd, :], start=True, stop=True)
                ins.then_inc(s["op"], 1)
            e.wait_ge(s["in_wo"], 16)
            for hd in range(NH):
                if hd % 4 == 0:
                    e.wait_ge(s["oT"], hd // 4 + 1)
                ins = mm(PB[4][:, 0:D], oT[:, hd, :], wo[:, hd, :], start=(hd == 0), stop=(hd == NH - 1))
            ins.then_inc(s["wop"], 1)
            turn_rows(2)
            e.wait_ge(s["in_gu"], 32)
            for g in range(4):
                for k in range(KD):
                    ins = mm(PB[g][:, :], hT[:, k, :], wgu[:, k, g * 512:(g + 1) * 512], start=(k == 0), stop=(k == KD - 1))
                ins.then_inc(s["gup"], 1)
            for g in range(2):
                e.wait_ge(s["mid"], g + 1)
                for u in range(4):
                    ins = tr(PB[5 + g][:, u * P:(u + 1) * P], mid[:, (4 * g + u) * P:(4 * g + u + 1) * P], eye)
                ins.then_inc(s["mTp"], 1)
            e.wait_ge(s["in_d"], 16)
            e.wait_ge(s["mT"], 2)
            for k in range(FF // P):
                ins = mm(PB[4][:, 0:D], midT[:, k, :], wd[:, k, :], start=(k == 0), stop=(k == FF // P - 1))
            ins.then_inc(s["dp"], 1)
            e.wait_ge(s["delta"], 1)
            for g in range(4):
                for u in range(2):
                    ins = mm(PB[g][:, u * D:(u + 1) * D], ET[:, 2 * g + u, :], hh[:, :], start=True, stop=True)
                ins.then_inc(s["scp"], 1)

        @block.scalar
        def _(e):
            f = e.activation
            e.wait_ge(s["gathered"], 1)
            f(xs[:, :], PB[2][:, 0:D], ACT.Copy).then_inc(s["xs"], 1)
            f(cossin[:, :, :], PB[3][:, 0:2 * HD].rearrange("p (a b) -> p a b", a=2), ACT.Copy).then_inc(s["xs"], 1)
            e.wait_ge(s["xs"], 1)
            f(sq[:, :], xs[:, :], ACT.Square, accum_out=ms[:, 0:1]).then_inc(s["ss"], 1)
            for g in range(2):
                e.wait_ge(s["ETp"], g + 1)
                f(ET[:, 4 * g:4 * g + 4, :], bank4(g), ACT.Copy).then_inc(s["ET"], 1)
            e.wait_ge(s["hTp"], 1)
            f(hT[:, :, :], PB[7][:, 0:D].rearrange("p (a b) -> p a b", a=KD), ACT.Copy).then_inc(s["hT"], 1)
            for g in range(6):
                e.wait_ge(s["trp"], g + 1)
                f(qkT[:, 4 * g:4 * g + 4, :], bank4(g), ACT.Copy).then_inc(s["tre"], 1)
            for g in range(4):
                e.wait_ge(s["mx"], g + 1)
                for u in range(4):
                    hd = 4 * g + u
                    f(att[:, hd, :], att[:, hd, :], ACT.Exp, bias=mx[:, hd:hd + 1], accum_out=sm[:, hd:hd + 1]).then_inc(s["exp"], 1)
            for g in range(4):
                e.wait_ge(s["pTp"], g + 1)
                f(attT[:, 4 * g:4 * g + 4, :], bank4(4 + g), ACT.Copy).then_inc(s["pT"], 1)
            for g in range(4):
                e.wait_ge(s["op"], g + 1)
                f(oT[:, 4 * g:4 * g + 4, :], bank4(g), ACT.Copy).then_inc(s["oT"], 1)
            e.wait_ge(s["x1"], 1)
            f(sq[:, :], x1[:, :], ACT.Square, accum_out=ms[:, 2:3]).then_inc(s["ss"], 1)
            e.wait_ge(s["hTp"], 2)
            f(hT[:, :, :], PB[7][:, 0:D].rearrange("p (a b) -> p a b", a=KD), ACT.Copy).then_inc(s["hT"], 1)
            for g in range(2):
                e.wait_ge(s["gup"], g + 1)
                f(mid[:, g * 512:(g + 1) * 512], PB[g][:, :], ACT.Silu).then_inc(s["silu"], 1)
            for g in range(2):
                e.wait_ge(s["mTp"], g + 1)
                f(midT[:, 4 * g:4 * g + 4, :], bank4(5 + g), ACT.Copy).then_inc(s["mT"], 1)
            e.wait_ge(s["gate"], 1)
            f(gate[:, :], gate[:, :], ACT.Sigmoid).then_inc(s["gate"], 1)

        @block.vector
        def _(e):
            tt, ts, stt = e.tensor_tensor, e.tensor_scalar, e.scalar_tensor_tensor
            ch = Chain(e, s["v"])
            ln.vector(ch, xres, h, 1, s["h"])
            e.wait_ge(s["in_a"], 64)
            e.wait_ge(s["h"], NT)
            ch.link(tt(prod[:, :, :], h[:, :, :], over(wr[:, :], NT), ALU.mult))
            e.tensor_reduce(sc[:, :], prod[:, :, :], AX.X, ALU.add).then_inc(s["sc"], 1)
            e.wait_ge(s["rowT"], 1)
            ch.link(e.tensor_copy(row[:, :], PB[0][0:B, 0:T]))
            src = row
            for k in range(TOP // 8):
                dst = work[k % 2]
                ch.link(e.max(top8[:, 8 * k:8 * k + 8], src[:, :]))
                ch.link(e.match_replace(dst[:, :], top8[:, 8 * k:8 * k + 8], src[:, :], -3.0e38))
                src = dst
            ch.link(tt(mask[:, :], src[:, :], row[:, :], ALU.not_equal))
            ch.link(e.tensor_tensor_scan(pos[:, :], mask[:, :], mask[:, :], 0.0, ALU.add, ALU.max))
            ch.link(stt(out=pos[:, :], in0=pos[:, :], scalar=cst("slot0")[0:B, :], in1=mask[:, :], op0=ALU.add, op1=ALU.mult))
            ts(pos[:, :], pos[:, :], -1.0, None, ALU.add).then_inc(s["code"], 1)
            e.wait_ge(s["slotT"], 1)
            ch.link(e.tensor_copy(slot[:, :].rearrange("p (b c) -> p c b", c=2), PB[1][:, 0:NT].rearrange("p (c b) -> p c b", c=2)))
            for t in range(NT):
                ts(E_[:, t, :], cst("count"), slot[:, t:t + 1], None, ALU.is_equal).then_inc(s["E"], 1)

            e.wait_ge(s["xs"], 2)
            ch.link(tt(prod[:, 0, :], xs[:, :], wr[:, :], ALU.mult))
            e.tensor_reduce(gate[:, :], prod[:, 0, :], AX.X, ALU.add).then_inc(s["gate"], 1)

            def rms(k, x):
                e.wait_ge(s["ss"], k)
                ts(ms[:, 2 * k - 1:2 * k], ms[:, 2 * k - 2:2 * k - 1], 1.0 / D, RMS_EPS, ALU.mult, ALU.add).then_inc(s["rms"], 1)
                e.wait_ge(s["rms"], 2 * k)
                stt(out=hh[:, :], in0=x[:, :], scalar=ms[:, 2 * k - 2:2 * k - 1], in1=lnw[:, k - 1, :], op0=ALU.mult, op1=ALU.mult)\
                    .then_inc(s["hh"], 1)

            rms(1, xs)
            for g in range(8):
                e.wait_ge(s["qkvp"], g + 1)
                tt(qkv[:, 4 * g:4 * g + 4, :], bank4(g), bias[:, g * 512:(g + 1) * 512].rearrange("p (a b) -> p a b", a=4), ALU.add)\
                    .then_inc(s["qkv"], 1)
            e.wait_ge(s["qkv"], 8)
            e.wait_ge(s["rope_g"], 1)
            for a, b in ((0, NH), (NH, NH + NKV)):
                ch.link(tt(qkv[:, a:b, :], qkv[:, a:b, :], over(cossin[:, 0, :], b - a), ALU.mult))
                tt(qkv[:, a:b, :], qkv[:, a:b, :], rot[:, a:b, :], ALU.add).then_inc(s["rope"], 1)
            for g in range(4):
                e.wait_ge(s["sp"], g + 1)
                q = slice(4 * g, 4 * g + 4)
                ch.link(stt(out=att[:, q, :], in0=bank4(g), scalar=HD ** -0.5, in1=over(cst("causal"), 4), op0=ALU.mult, op1=ALU.add))
                ch.link(e.tensor_reduce(mx[:, q], att[:, q, :], AX.X, ALU.max))
                ts(mx[:, q], mx[:, q], -1.0, None, ALU.mult).then_inc(s["mx"], 1)
            e.wait_ge(s["exp"], NH)
            ch.link(e.reciprocal(sm[:, :], sm[:, :]))
            for hd in range(NH):
                ts(att[:, hd, :], att[:, hd, :], sm[:, hd:hd + 1], None, ALU.mult).then_inc(s["nrm"], 1)
            e.wait_ge(s["wop"], 1)
            tt(x1[:, :], PB[4][:, 0:D], xs[:, :], ALU.add).then_inc(s["x1"], 1)
            e.wait_ge(s["x1"], 1)
            rms(2, x1)
            for g in range(2):
                e.wait_ge(s["gup"], g + 3)
                e.wait_ge(s["silu"], g + 1)
                q = slice(g * 512, (g + 1) * 512)
                tt(mid[:, q], mid[:, q], PB[2 + g][:, :], ALU.mult).then_inc(s["mid"], 1)
            e.wait_ge(s["dp"], 1)
            ch.link(tt(x1[:, :], x1[:, :], PB[4][:, 0:D], ALU.add))
            ch.link(tt(x1[:, :], x1[:, :], xs[:, :], ALU.subtract))
            e.wait_ge(s["gate"], 2)
            ts(hh[:, :], x1[:, :], gate[:, 0:1], None, ALU.mult).then_inc(s["delta"], 1)
            for g in range(4):
                e.wait_ge(s["scp"], g + 1)
                q = slice(2 * g, 2 * g + 2)
                ch.add(tt(h[:, q, :], h[:, q, :], PB[g][:, :].rearrange("p (a b) -> p a b", a=2), ALU.add))
            ch.wait()
            ln.vector(ch, h, prod, 2, s["ln2"])
            e.wait_ge(s["ln2"], NT)
            tt(xres[:, :, :], xres[:, :, :], prod[:, :, :], ALU.add).then_inc(s["fin"], 1)
            e.wait_ge(s["fin"], 1)

        @block.gpsimd
        def _(e):
            tt = e.tensor_tensor
            ch = Chain(e, s["g"])
            ln.pool(ch, 1)
            mh = cst("mhalf")
            for k in (1, 2):
                e.wait_ge(s["rms"], 2 * k - 1)
                tt(ms[:, 2 * k - 2:2 * k - 1], ms[:, 2 * k - 1:2 * k], mh[:, 0:1], ALU.pow).then_inc(s["rms"], 1)
                if k == 1:
                    e.wait_ge(s["xs"], 2)
                    n, hf = NH + NKV, HD // 2
                    e.wait_ge(s["qkv"], 6)
                    ch.add(tt(rot[:, :, 0:hf], qkv[:, 0:n, hf:HD], over(cossin[:, 1, 0:hf], n), ALU.mult))
                    tt(rot[:, :, hf:HD], qkv[:, 0:n, 0:hf], over(cossin[:, 1, hf:HD], n), ALU.mult).then_inc(s["rope_g"], 1)
            ln.pool(ch, 2)


def stage_linear(nc, m, A):
    with ExitStack() as ctx:
        sb = lambda n, s, d=F32: ctx.enter_context(nc.sbuf_tensor("l_" + n, s, d))
        sem = lambda n: nc.alloc_semaphore("l_" + n)
        PB, C, xres = m["PB"], m["C"], m["xres"]

        def cst(name):
            a, b = CONST_AT[name]
            return C[:, a:b]

        eye = cst("eye")
        ln = RowNorm(ctx, nc, "l_", cst("mhalf"))
        h = sb("h", [P, NT, D])
        W = sb("W", [P, 5, KD, D])
        sq = sb("sq", [P, NT, D])
        ms = sb("ms", [P, 2, NT])
        xT = sb("xT", [P, KD, B * T])
        qkg = sb("qkg", [P, 3, KD, B * T])
        v_ = sb("v", [P, NT, D])
        ST = sb("ST", [P, B, 3, P])
        oT = sb("oT", [P, KD, B * T])

        names = ["in", "v", "g", "a", "h", "sq", "ms", "root", "xn", "tp", "xT", "pp", "pe", "sp", "S", "op", "o", "fp", "f", "ln2", "fin"]
        s = {n: sem(n) for n in names}
        block = ctx.enter_context(nc.Block())

        @block.sync
        def _(e):
            for k, name in enumerate(("q", "k", "g", "v", "p")):
                e.dma_start(W[:, k, :, :], A[f"W{name}_t"].rearrange("(k p) n -> p k n", p=P)).then_inc(s["in"], 16)

        @block.tensor
        def _(e):
            mm, tr = e.matmul, e.transpose
            for t in range(NT):
                e.wait_ge(s["xn"], t + 1)
                for k in range(KD):
                    ins = tr(PB[t // 2][:, (t % 2) * 256 + k * P:(t % 2) * 256 + (k + 1) * P], sq[:, t, k * P:(k + 1) * P], eye)
                ins.then_inc(s["tp"], 1)
            e.wait_ge(s["in"], 80)
            n = 0
            for w in range(3):
                for o in range(KD):
                    for hf in range(2):
                        e.wait_ge(s["xT"], 4 if n >= 2 or hf else 2)
                        bank = PB[(4 + n) % 8]
                        if n >= 4:
                            e.wait_ge(s["xT"], 4)
                        if n >= 8:
                            e.wait_ge(s["pe"], n - 7)
                        for k in range(KD):
                            ins = mm(bank[:, :], W[:, w, k, o * P:(o + 1) * P], xT[:, k, hf * 512:(hf + 1) * 512], start=(k == 0), stop=(k == KD - 1))
                        ins.then_inc(s["pp"], 1)
                        n += 1
            for g in range(4):
                e.wait_ge(s["pe"], n - 7)
                for u in range(2):
                    t = 2 * g + u
                    for k in range(KD):
                        ins = mm(PB[(4 + n) % 8][:, u * 256:(u + 1) * 256], xT[:, k, t * P:(t + 1) * P], W[:, 3, k, :], start=(k == 0), stop=(k == KD - 1))
                ins.then_inc(s["pp"], 1)
                n += 1
            e.wait_ge(s["pe"], 16)
            for b in range(B):
                q0 = b * T
                for k in range(KD):
                    mm(PB[4 + b][:, 0:256], qkg[:, 1, k, q0:q0 + P], qkg[:, 0, k, q0:q0 + T], start=(k == 0), stop=(k == KD - 1))
                for k in range(KD):
                    ins = mm(PB[4 + b][:, 256:384], qkg[:, 1, k, q0 + P:q0 + T], qkg[:, 0, k, q0 + P:q0 + T], start=(k == 0), stop=(k == KD - 1))
                ins.then_inc(s["sp"], 1)
            for b in range(B):
                e.wait_ge(s["S"], b + 1)
                for o in range(KD):
                    mm(PB[b][:, o * 256:o * 256 + 256], v_[:, 2 * b, o * P:(o + 1) * P], ST[:, b, 0:2, :].rearrange("p a b -> p (a b)"), start=True, stop=False)
                    ins = mm(PB[b][:, o * 256 + P:o * 256 + 256], v_[:, 2 * b + 1, o * P:(o + 1) * P], ST[:, b, 2, :], start=False, stop=True)
                ins.then_inc(s["op"], 1)
            for b in range(B):
                e.wait_ge(s["o"], b + 1)
                for u in range(2):
                    t = 2 * b + u
                    for o in range(KD):
                        ins = mm(PB[4 + b][:, u * 256:(u + 1) * 256], oT[:, o, t * P:(t + 1) * P], W[:, 4, o, :], start=(o == 0), stop=(o == KD - 1))
                ins.then_inc(s["fp"], 1)

        @block.scalar
        def _(e):
            f = e.activation
            for g in range(4):
                e.wait_ge(s["tp"], 2 * g + 2)
                for u in range(2):
                    t = 2 * g + u
                    ins = f(xT[:, :, t * P:(t + 1) * P], PB[g][:, u * 256:(u + 1) * 256].rearrange("p (k t) -> p k t", k=KD), ACT.Copy)
                ins.then_inc(s["xT"], 1)
            n = 0
            for w in range(3):
                for o in range(KD):
                    for hf in range(2):
                        e.wait_ge(s["pp"], n + 1)
                        f(qkg[:, w, o, hf * 512:(hf + 1) * 512], PB[(4 + n) % 8][:, :], ACT.Silu if w < 2 else ACT.Sigmoid).then_inc(s["pe"], 1)
                        n += 1
            for g in range(4):
                e.wait_ge(s["pp"], n + 1)
                f(v_[:, 2 * g:2 * g + 2, :], PB[(4 + n) % 8][:, :].rearrange("p (a b) -> p a b", a=2), ACT.Silu).then_inc(s["pe"], 1)
                n += 1

        @block.vector
        def _(e):
            tt, ts = e.tensor_tensor, e.tensor_scalar
            ch = Chain(e, s["v"])
            ln.vector(ch, xres, h, 1, s["h"])
            e.wait_ge(s["h"], NT)
            ch.link(tt(sq[:, :, :], h[:, :, :], h[:, :, :], ALU.mult))
            ch.link(e.tensor_reduce(ms[:, 0, :], sq[:, :, :], AX.X, ALU.add))
            ts(ms[:, 1, :], ms[:, 0, :], 1.0 / D, float(np.finfo(np.float32).eps), ALU.mult, ALU.add).then_inc(s["ms"], 1)
            e.wait_ge(s["root"], 1)
            for t in range(NT):
                ts(sq[:, t, :], h[:, t, :], ms[:, 0, t:t + 1], None, ALU.mult).then_inc(s["xn"], 1)
            e.wait_ge(s["pe"], 16)
            for b in range(B):
                e.wait_ge(s["sp"], b + 1)
                tt(ST[:, b, :, :], PB[4 + b][:, 0:384].rearrange("p (a b) -> p a b", a=3), cst("lmask").rearrange("p (a b) -> p a b", a=3), ALU.mult)\
                    .then_inc(s["S"], 1)
            for b in range(B):
                e.wait_ge(s["op"], b + 1)
                tt(oT[:, :, b * T:(b + 1) * T], PB[b][:, :].rearrange("p (a b) -> p a b", a=KD), qkg[:, 2, :, b * T:(b + 1) * T], ALU.mult)\
                    .then_inc(s["o"], 1)
            for b in range(B):
                e.wait_ge(s["fp"], b + 1)
                ch.add(e.tensor_copy(h[:, 2 * b:2 * b + 2, :], PB[4 + b][:, :].rearrange("p (a b) -> p a b", a=2)))
            ch.wait()
            ln.vector(ch, h, sq, 2, s["ln2"])
            e.wait_ge(s["ln2"], NT)
            tt(xres[:, :, :], xres[:, :, :], sq[:, :, :], ALU.add).then_inc(s["fin"], 1)
            e.wait_ge(s["fin"], 1)

        @block.gpsimd
        def _(e):
            ch = Chain(e, s["g"])
            ln.pool(ch, 1)
            e.wait_ge(s["ms"], 1)
            e.tensor_tensor(ms[:, 0, :], ms[:, 1, :], cst("mhalf")[:, 0:NT], ALU.pow).then_inc(s["root"], 1)
            ln.pool(ch, 2)


NSH, NRT, ED = 2, 16, 128


def stage_experts(nc, m, A):
    with ExitStack() as ctx:
        sb = lambda n, s, d=F32: ctx.enter_context(nc.sbuf_tensor("e_" + n, s, d))
        sem = lambda n: nc.alloc_semaphore("e_" + n)
        PB, C, xres = m["PB"], m["C"], m["xres"]

        def cst(name):
            a, b = CONST_AT[name]
            return C[:, a:b]

        eye = cst("eye")
        ln = RowNorm(ctx, nc, "e_", cst("mhalf"))
        h = sb("h", [P, NT, D])
        acc = sb("acc", [P, NT, D])
        xT = sb("xT", [P, KD, B * T])
        wrt = sb("wrt", [P, KD, NRT])
        up = [sb(f"up{i}", [P, KD, ED]) for i in range(2)]
        down = [sb(f"down{i}", [P, D]) for i in range(2)]
        midT = [sb(f"midT{i}", [P, B * T]) for i in range(2)]
        pr = sb("pr", [P, NT, NRT])
        mx = sb("mx", [P, NT])
        sm = sb("sm", [P, NT])
        top8 = sb("top8", [P, NT, 8])
        idx = sb("idx", [P, NT, 8], U32)
        idf = sb("idf", [P, NT, 8])
        hot = sb("hot", [P, NT, NRT])
        gates = sb("gates", [P, NT, NRT])
        ge = [sb(f"ge{i}", [P, NT]) for i in range(2)]

        names = ["in", "wu0", "wu1", "wd0", "wd1", "v", "g", "a", "h", "tp", "xT", "rp", "sub", "exp", "gates", "ge", "up", "gelu", "down", "acc", "ln2", "fin", "out", "scal"]
        s = {n: sem(n) for n in names}
        NE = NSH + NRT
        block = ctx.enter_context(nc.Block())

        def one(ap, r):
            return ap[r:r + 1] if isinstance(r, int) else ap[bass.ds(r, 1)]

        @block.sync
        def _(e):
            e.dma_start(wrt[:, :, :], A["L1_ffn_W_router"].rearrange("(k p) n -> p k n", p=P)).then_inc(s["in"], 16)

            def source(n, which):
                shared = isinstance(n, int) and n < NSH
                kind, r = ("sh", n) if shared else ("rt", n - NSH)
                return one(A[f"L1_ffn_W{kind}_{which}"], r)

            def load_up(n, par):
                if not (isinstance(n, int) and n < 2):
                    e.wait_ge(s["up"], 2 * (n - 1))
                e.dma_start(up[par][:, :, :], source(n, "up").rearrange("e (k p) n -> p (e k) n", p=P)).then_inc(s[f"wu{par}"], 16)

            def load_down(n, par):
                if not (isinstance(n, int) and n < 2):
                    e.wait_ge(s["down"], 4 * (n - 1))
                e.dma_start(down[par][:, :], source(n, "down").rearrange("e p n -> p (e n)")).then_inc(s[f"wd{par}"], 16)

            load_up(0, 0)
            load_up(1, 1)
            load_down(0, 0)
            load_up(2, 0)
            load_down(1, 1)
            load_up(3, 1)
            with e.Fori(1, NE // 2 - 1) as i:
                load_down(2 * i, 0)
                load_up(2 * i + 2, 0)
                load_down(2 * i + 1, 1)
                load_up(2 * i + 3, 1)
            load_down(NE - 2, 0)
            load_down(NE - 1, 1)
            e.wait_ge(s["fin"], 1)
            e.dma_start(A["o"].rearrange("b (c p) d -> p (b c) d", p=P), xres[:, :, :]).then_inc(s["out"], 16)
            e.wait_ge(s["out"], 16)

        @block.tensor
        def _(e):
            mm, tr = e.matmul, e.transpose
            for t in range(NT):
                e.wait_ge(s["h"], t + 1)
                for k in range(KD):
                    ins = tr(PB[t // 2][:, (t % 2) * 256 + k * P:(t % 2) * 256 + (k + 1) * P], h[:, t, k * P:(k + 1) * P], eye)
                ins.then_inc(s["tp"], 1)
            e.wait_ge(s["in"], 16)
            e.wait_ge(s["xT"], 4)
            for t in range(NT):
                for k in range(KD):
                    ins = mm(PB[4][:, t * NRT:(t + 1) * NRT], xT[:, k, t * P:(t + 1) * P], wrt[:, k, :], start=(k == 0), stop=(k == KD - 1))
            ins.then_inc(s["rp"], 1)

            def up_step(n, par):
                e.wait_ge(s[f"wu{par}"], 8 * (n - par) + 16)
                if not (isinstance(n, int) and n < 2):
                    e.wait_ge(s["gelu"], 2 * (n - 1))
                for hf in range(2):
                    for k in range(KD):
                        ins = mm(PB[2 * par + hf][:, :], up[par][:, k, :], xT[:, k, hf * 512:(hf + 1) * 512], start=(k == 0), stop=(k == KD - 1))
                    ins.then_inc(s["up"], 1)

            def down_step(n, par):
                e.wait_ge(s[f"wd{par}"], 8 * (n - par) + 16)
                for g in range(4):
                    if isinstance(n, int) and n == 0:
                        e.wait_ge(s["sub"], 1)
                    else:
                        e.wait_ge(s["acc"], 4 * n - 3 + g)
                    e.wait_ge(s["gelu"], 2 * n + 1 + g // 2)
                    for u in range(2):
                        t = 2 * g + u
                        ins = mm(PB[4 + g][:, u * D:(u + 1) * D], midT[par][:, t * P:(t + 1) * P], down[par][:, :], start=True, stop=True)
                    ins.then_inc(s["down"], 1)

            up_step(0, 0)
            up_step(1, 1)
            down_step(0, 0)
            with e.Fori(1, NE // 2) as i:
                up_step(2 * i, 0)
                down_step(2 * i - 1, 1)
                up_step(2 * i + 1, 1)
                down_step(2 * i, 0)
            down_step(NE - 1, 1)

        @block.scalar
        def _(e):
            f = e.activation
            for g in range(4):
                e.wait_ge(s["tp"], 2 * g + 2)
                for u in range(2):
                    t = 2 * g + u
                    ins = f(xT[:, :, t * P:(t + 1) * P], PB[g][:, u * 256:(u + 1) * 256].rearrange("p (k t) -> p k t", k=KD), ACT.Copy)
                ins.then_inc(s["xT"], 1)
            e.wait_ge(s["sub"], 2)
            f(pr[:, :, :], pr[:, :, :], ACT.Exp).then_inc(s["exp"], 1)

            def gelu(n, par):
                for hf in range(2):
                    e.wait_ge(s["up"], 2 * n + hf + 1)
                    if not (isinstance(n, int) and n < 2):
                        e.wait_ge(s["down"], 4 * (n - 1))
                    f(midT[par][:, hf * 512:(hf + 1) * 512], PB[2 * par + hf][:, :], ACT.Gelu).then_inc(s["gelu"], 1)

            gelu(0, 0)
            gelu(1, 1)
            with e.Fori(1, NE // 2) as i:
                gelu(2 * i, 0)
                gelu(2 * i + 1, 1)

        @block.vector
        def _(e):
            tt, ts, stt = e.tensor_tensor, e.tensor_scalar, e.scalar_tensor_tensor
            ch = Chain(e, s["v"])
            ln.vector(ch, xres, h, 1, s["h"])
            e.wait_ge(s["rp"], 1)
            logits = PB[4][:, 0:NT * NRT].rearrange("p (t n) -> p t n", n=NRT)
            ch.link(e.tensor_reduce(mx[:, :], logits, AX.X, ALU.max))
            tt(pr[:, :, :], logits, along(mx[:, :], NRT), ALU.subtract).then_inc(s["sub"], 2)
            e.wait_ge(s["exp"], 1)
            ch.link(e.tensor_reduce(sm[:, :], pr[:, :, :], AX.X, ALU.add))
            ch.link(e.reciprocal(sm[:, :], sm[:, :]))
            ch.link(tt(pr[:, :, :], pr[:, :, :], along(sm[:, :], NRT), ALU.mult))
            for t in range(NT):
                ch.add(e.max(top8[:, t, :], pr[:, t, :]))
            ch.wait()
            for t in range(NT):
                ch.add(e.max_index(idx[:, t, :], top8[:, t, :], pr[:, t, :]))
            ch.wait()
            ch.link(e.tensor_copy(idf[:, :, :], idx[:, :, :]))
            num = cst("count")[:, 0:NRT]
            for t in range(NT):
                ch.add(ts(hot[:, t, :], num, idf[:, t, 0:1], top8[:, t, 0:1], ALU.is_equal, ALU.mult))
                ch.add(ts(gates[:, t, :], num, idf[:, t, 1:2], top8[:, t, 1:2], ALU.is_equal, ALU.mult))
            ch.wait()
            tt(gates[:, :, :], gates[:, :, :], hot[:, :, :], ALU.add).then_inc(s["gates"], 1)
            e.wait_ge(s["gates"], 1)

            def add(n, par):
                shared = isinstance(n, int) and n < NSH
                if not shared:
                    src = gates[:, :, n - NSH:n - NSH + 1] if isinstance(n, int) else gates[:, :, bass.ds(n - NSH, 1)]
                    e.wait_ge(s["acc"], 4 * n)
                    e.tensor_copy(ge[par][:, :], src.rearrange("p t n -> p (t n)")).then_inc(s["ge"], 1)
                    e.wait_ge(s["ge"], n - NSH + 1)
                for g in range(4):
                    e.wait_ge(s["down"], 4 * n + g + 1)
                    if not (isinstance(n, int) and n == 0) and shared:
                        e.wait_ge(s["acc"], 4 * n - 3 + g)
                    q = slice(2 * g, 2 * g + 2)
                    src = PB[4 + g][:, :].rearrange("p (a b) -> p a b", a=2)
                    if shared:
                        ins = e.tensor_copy(acc[:, q, :], src) if n == 0 else tt(acc[:, q, :], acc[:, q, :], src, ALU.add)
                    else:
                        for u in range(2):
                            t = 2 * g + u
                            ins = stt(out=acc[:, t, :], in0=src[:, u, :], scalar=ge[par][:, t:t + 1], in1=acc[:, t, :], op0=ALU.mult, op1=ALU.add)
                    ins.then_inc(s["acc"], 1)

            add(0, 0)
            add(1, 1)
            with e.Fori(1, NE // 2) as i:
                add(2 * i, 0)
                add(2 * i + 1, 1)
            e.wait_ge(s["acc"], 4 * NE)
            ln.vector(ch, acc, h, 2, s["ln2"])
            e.wait_ge(s["ln2"], NT)
            tt(xres[:, :, :], xres[:, :, :], h[:, :, :], ALU.add).then_inc(s["fin"], 1)

        @block.gpsimd
        def _(e):
            ch = Chain(e, s["g"])
            ln.pool(ch, 1)
            ln.pool(ch, 2)


def build_program(nc, A):
    with ExitStack() as ctx:
        m = {"PB": [ctx.enter_context(nc.psum_tensor(f"bank{i}", [P, 512], F32)) for i in range(8)],
             "C": ctx.enter_context(nc.sbuf_tensor("constants", [P, A["const"].shape[1]], F32)),
             "xres": ctx.enter_context(nc.sbuf_tensor("residual", [P, NT, D], F32))}
        for stage in (stage_delta, stage_top, stage_linear, stage_experts):
            with nc.cleanup_on_exit():
                stage(nc, m, A)
                nc.all_engine_barrier()
            nc.all_engine_barrier()


def conv_by_head(w):
    w = w.reshape(-1, TAPS)
    q = w[:NK * DK].reshape(NK, 1, DK, TAPS)
    k = w[NK * DK:2 * NK * DK].reshape(NK, 1, DK, TAPS)
    v = w[2 * NK * DK:].reshape(NK, RF, DK, TAPS)
    return np.concatenate([q, k, v], 1).transpose(0, 2, 1, 3).reshape(NK, DK, 4 * TAPS)


def rope_table():
    inv = (1.0 / np.float32(ROPE_THETA) ** (np.arange(0, HD, 2, dtype=np.float32) / np.float32(HD))).astype(np.float32)
    ang = np.arange(T, dtype=np.float32)[:, None] * inv
    cos, sin = np.cos(ang), np.sin(ang)
    return np.concatenate([cos, cos, -sin, sin], 1).astype(np.float32)


_PLAIN = ["L0_attn_hidden_states", "L0_attn_w_qkvz", "L0_attn_w_ba", "L0_attn_dt_bias", "L0_attn_A_log", "L0_attn_norm_w", "L0_attn_w_out",
          "L0_ffn_w_router", "L0_ffn_wq", "L0_ffn_bq", "L0_ffn_wk", "L0_ffn_bk", "L0_ffn_wv", "L0_ffn_bv", "L0_ffn_wo", "L0_ffn_w_gate",
          "L0_ffn_w_up", "L0_ffn_w_down", "L0_ffn_ln1_w", "L0_ffn_ln2_w", "L1_ffn_Wsh_up", "L1_ffn_Wsh_down", "L1_ffn_Wrt_up",
          "L1_ffn_Wrt_down", "L1_ffn_W_router"]


def kernel(**inputs):
    import concourse.bacc as _bacc
    from concourse.bass_utils import run_bass_kernel_spmd as _run

    arrays = {name: np.ascontiguousarray(inputs[name]) for name in _PLAIN}
    arrays["conv_r"] = np.ascontiguousarray(conv_by_head(np.asarray(inputs["L0_attn_conv_w"])))
    for w in "qkvgp":
        arrays[f"W{w}_t"] = np.ascontiguousarray(np.asarray(inputs[f"L1_attn_W{w}"]).T)
    arrays["const"] = packed_constants()[0]
    arrays["rope"] = rope_table()

    nc = _bacc.Bacc("TRN2", target_bir_lowering=False, num_devices=1)
    A = {k: nc.dram_tensor(k, a.shape, mybir.dt.from_np(a.dtype), kind="ExternalInput").ap() for k, a in arrays.items()}
    A["o"] = nc.dram_tensor("out", (B, T, D), F32, kind="ExternalOutput").ap()
    build_program(nc, A)
    r = _run(nc, [arrays], core_ids=[0])
    return r.results[0]["out"]
```
